# Optimizing a Trainium2 kernel written in Bass

```python
import numpy as np
import jax
import jax.numpy as jnp

def _softmax(x, axis=-1):
    return jax.nn.softmax(x, axis=axis)

def _gelu(x):
    return jax.nn.gelu(x, approximate=True)

def _silu(x):
    return jax.nn.silu(x)

def _sigmoid(x):
    return jax.nn.sigmoid(x)

def _layernorm(x, axis=-1, eps=1e-05):
    m = jnp.mean(x, axis=axis, keepdims=True)
    v = jnp.var(x, axis=axis, keepdims=True)
    return (x - m) / jnp.sqrt(v + eps)

def _scatter_add(tgt, idx, src, axis=0):
    return tgt.at[idx].add(src)

def _segment_sum(src, seg, n):
    return jax.ops.segment_sum(src, seg, n)
kernel_name = 'mk_gnn_preln_d1_gnn_r32_f8d3ec'

def setup_inputs(seed: int=0):
    np.random.seed(seed)
    _w = jnp.asarray

    def _rec_inputs():
        import jax
        import jax.numpy as jnp
        _gk = jax.random.key(seed)
        x = -0.000202 + 1 * jax.random.normal(jax.random.fold_in(_gk, 1), (50000, 128), jnp.float32)
        src = jax.random.randint(jax.random.fold_in(_gk, 2), (25000,), 0, 50000, jnp.int32)
        dst = jax.random.randint(jax.random.fold_in(_gk, 3), (25000,), 0, 50000, jnp.int32)
        _o = jnp.argsort(dst, stable=True)
        src = src[_o]
        dst = dst[_o]
        return (x, src, dst)
    x, src, dst = _rec_inputs()

    def _L0_gnn_setup():
        import jax, jax.numpy as jnp
        import numpy as np
        N_NODES = 50000
        LN_EPS = 1e-05
        NEG_SLOPE = 0.01

        def _leaky(x):
            return jnp.where(x >= 0, x, NEG_SLOPE * x)

        def _layer_norm(x, g, b):
            mu = jnp.mean(x, axis=-1, keepdims=True)
            var = jnp.mean(jnp.square(x - mu), axis=-1, keepdims=True)
            return (x - mu) * jax.lax.rsqrt(var + LN_EPS) * g + b

        def _edge_conv(x, src, dst, W1, b1, W2, b2):
            x_i = x[dst]
            x_j = x[src]
            h = jnp.concatenate([x_i, x_j - x_i], axis=-1)
            m = _leaky(h @ W1 + b1) @ W2 + b2
            return jax.ops.segment_sum(m, dst, num_segments=N_NODES)
        key = jax.random.key(seed)
        ks = jax.random.split(key, 8)
        din, hid, E = (128, 128, 25000)

        def kaiming(k, fan_in, shape):
            gain = np.sqrt(2.0 / (1.0 + 0.01 ** 2))
            bound = gain * np.sqrt(3.0 / fan_in)
            return jax.random.uniform(k, shape, jnp.float32, -bound, bound)
        x = jax.random.normal(ks[0], (N_NODES, din), jnp.float32)
        edges = jax.random.randint(ks[1], (2, E), 0, N_NODES, jnp.int64)
        return {'task_features': x, 'task_edges': edges, 'W1_0': kaiming(ks[2], 2 * din, (2 * din, hid)), 'b1_0': jnp.zeros((hid,), jnp.float32), 'W2_0': kaiming(ks[3], hid, (hid, hid)), 'b2_0': jnp.zeros((hid,), jnp.float32), 'ln_g0': jnp.ones((hid,), jnp.float32), 'ln_b0': jnp.zeros((hid,), jnp.float32), 'W1_1': kaiming(ks[4], 2 * hid, (2 * hid, hid)), 'b1_1': jnp.zeros((hid,), jnp.float32), 'W2_1': kaiming(ks[5], hid, (hid, hid)), 'b2_1': jnp.zeros((hid,), jnp.float32), 'ln_g1': jnp.ones((hid,), jnp.float32), 'ln_b1': jnp.zeros((hid,), jnp.float32)}
    _L0_gnn_all = _L0_gnn_setup()
    _L0_gnn_in = {k: v for k, v in _L0_gnn_all.items() if k in ('W1_0', 'b1_0', 'W2_0', 'b2_0', 'ln_g0', 'ln_b0', 'W1_1', 'b1_1', 'W2_1', 'b2_1', 'ln_g1', 'ln_b1')}
    del _L0_gnn_all
    return {'x': x, 'src': src, 'dst': dst, 'L0_gnn_W1_0': _L0_gnn_in['W1_0'], 'L0_gnn_b1_0': _L0_gnn_in['b1_0'], 'L0_gnn_W2_0': _L0_gnn_in['W2_0'], 'L0_gnn_b2_0': _L0_gnn_in['b2_0'], 'L0_gnn_ln_g0': _L0_gnn_in['ln_g0'], 'L0_gnn_ln_b0': _L0_gnn_in['ln_b0'], 'L0_gnn_W1_1': _L0_gnn_in['W1_1'], 'L0_gnn_b1_1': _L0_gnn_in['b1_1'], 'L0_gnn_W2_1': _L0_gnn_in['W2_1'], 'L0_gnn_b2_1': _L0_gnn_in['b2_1'], 'L0_gnn_ln_g1': _L0_gnn_in['ln_g1'], 'L0_gnn_ln_b1': _L0_gnn_in['ln_b1']}

def reference(x, src, dst, L0_gnn_W1_0, L0_gnn_b1_0, L0_gnn_W2_0, L0_gnn_b2_0, L0_gnn_ln_g0, L0_gnn_ln_b0, L0_gnn_W1_1, L0_gnn_b1_1, L0_gnn_W2_1, L0_gnn_b2_1, L0_gnn_ln_g1, L0_gnn_ln_b1):
    import jax
    import jax.numpy as jnp

    def _L0_gnn_ref(task_features, task_edges, W1_0, b1_0, W2_0, b2_0, ln_g0, ln_b0, W1_1, b1_1, W2_1, b2_1, ln_g1, ln_b1):
        import jax, jax.numpy as jnp
        import numpy as np
        N_NODES = 50000
        LN_EPS = 1e-05
        NEG_SLOPE = 0.01

        def _leaky(x):
            return jnp.where(x >= 0, x, NEG_SLOPE * x)

        def _layer_norm(x, g, b):
            mu = jnp.mean(x, axis=-1, keepdims=True)
            var = jnp.mean(jnp.square(x - mu), axis=-1, keepdims=True)
            return (x - mu) * jax.lax.rsqrt(var + LN_EPS) * g + b

        def _edge_conv(x, src, dst, W1, b1, W2, b2):
            x_i = x[dst]
            x_j = x[src]
            h = jnp.concatenate([x_i, x_j - x_i], axis=-1)
            m = _leaky(h @ W1 + b1) @ W2 + b2
            return jax.ops.segment_sum(m, dst, num_segments=N_NODES)
        src, dst = (task_edges[0], task_edges[1])
        h = task_features
        h = _edge_conv(h, src, dst, W1_0, b1_0, W2_0, b2_0)
        h = _leaky(_layer_norm(h, ln_g0, ln_b0))
        h = _edge_conv(h, src, dst, W1_1, b1_1, W2_1, b2_1)
        h = _leaky(_layer_norm(h, ln_g1, ln_b1))
        return h
    edge_index = jnp.stack([src, dst])
    h = jnp.maximum(_layernorm(x, axis=-1), 0.0)
    x = x + _L0_gnn_ref(h, edge_index, L0_gnn_W1_0, L0_gnn_b1_0, L0_gnn_W2_0, L0_gnn_b2_0, L0_gnn_ln_g0, L0_gnn_ln_b0, L0_gnn_W1_1, L0_gnn_b1_1, L0_gnn_W2_1, L0_gnn_b2_1, L0_gnn_ln_g1, L0_gnn_ln_b1)
    return x

_drawn_inputs = setup_inputs


def setup_inputs(seed=0):
    import zlib

    import numpy as np

    out = dict(_drawn_inputs(seed))
    spreads = {'L0_gnn_b1_0': (0.0, 0.1),
     'L0_gnn_b2_0': (0.0, 0.1),
     'L0_gnn_ln_g0': (1.0, 0.2),
     'L0_gnn_ln_b0': (0.0, 0.1),
     'L0_gnn_b1_1': (0.0, 0.1),
     'L0_gnn_b2_1': (0.0, 0.1),
     'L0_gnn_ln_g1': (1.0, 0.2),
     'L0_gnn_ln_b1': (0.0, 0.1)}
    factors = {}
    for name, (base, spread) in spreads.items():
        noise = np.random.default_rng([zlib.crc32(name.encode()), seed]).standard_normal(out[name].shape)
        drawn = base * np.exp(spread * noise) if base else spread * noise
        out[name] = jnp.asarray(drawn.astype(out[name].dtype))
    for name, factor in factors.items():
        out[name] = (out[name] * factor).astype(out[name].dtype)
    return out
```

```python
from contextlib import ExitStack

import concourse.bass as bass
from concourse import mybir

F32 = mybir.dt.float32
I32 = mybir.dt.int32
ALU = mybir.AluOpType
ACT = mybir.ActivationFunctionType
AX = mybir.AxisListType

P = 128
EPS = 1e-5
SLOPE = 0.01


def build(nc, x, src, dst, weights, out):
    N, D = x.shape
    E = src.shape[0]
    NODE_TILES = -(-N // P)
    ROW = 2 * P
    PAIRS = -(-E // ROW)
    EDGE_TILES = 2 * PAIRS
    NPAD = -(-N // (4 * P)) * 4 * P
    SUM_TILES = NPAD // P + 1
    LAST = N - P

    h_dram = [nc.dram_tensor(f"h{l}_rows", [NPAD, D], F32, kind="Internal").ap() for l in range(2)]
    sums_dram = nc.dram_tensor("sums_rows", [SUM_TILES * P, D], F32, kind="Internal").ap()

    with ExitStack() as ctx:
        def sb(name, shape, dt=F32):
            return ctx.enter_context(nc.sbuf_tensor(name, shape, dt))

        def sem(name):
            return ctx.enter_context(nc.semaphore(name))

        ident = sb("ident", [P, P])
        ones_row = sb("ones_row", [1, P])
        eps_col = sb("eps_col", [P, 1])
        edge_rows = sb("edge_rows", [PAIRS, 2, ROW], I32)
        edge_rows_f = sb("edge_rows_f", [PAIRS, 2, ROW])
        dst_cols = sb("dst_cols", [P, EDGE_TILES])
        src_cols = sb("src_cols", [P, EDGE_TILES], I32)
        w1 = [sb(f"w1_{l}", [P, 2, D]) for l in range(2)]
        w1d = [sb(f"w1d_{l}", [P, D]) for l in range(2)]
        w2 = [sb(f"w2_{l}", [P, D]) for l in range(2)]
        vec_row = sb("vec_row", [1, 2, 4, D])
        vecs = sb("vecs", [P, 2, 4, D])
        psum = [ctx.enter_context(nc.psum_tensor(f"psum{i}", [P, 4, P], F32)) for i in range(8)]

        blanks_made = sem("blanks_made")
        masks_made = sem("masks_made")
        consts_set = sem("consts_set")
        edges_loaded = sem("edges_loaded")
        weights_loaded = sem("weights_loaded")
        edges_cast = sem("edges_cast")
        cols_made = sem("cols_made")
        waited = sem("waited")
        turned = sem("turned")
        setup_done = sem("setup_done")

        earlier = sb("earlier", [P, P])
        lane_dump = sb("lane_dump", [P, 1])
        g_rows = sb("g_rows", [P, 3, D])
        g_hT = sb("g_hT", [P, 2, P])
        g_hid = sb("g_hid", [P, 2, P])
        g_hidT = sb("g_hidT", [P, P])
        g_msg = sb("g_msg", [P, 2, D])
        g_key = sb("g_key", [P, P])
        g_same = sb("g_same", [P, 2, P])
        g_col = sb("g_col", [P, 2])
        g_idx = sb("g_idx", [P, 3], I32)
        g_node = sb("g_node", [P, 5, D])
        g_x = sb("g_x", [P, D])
        g_stats = sb("g_stats", [P, 6])
        g_mean = sb("g_mean", [P, 2])
        g_root = sb("g_root", [P, 2])
        g_zero = sb("g_zero", [P, D])

        node_in = [sem(f"node_in{k}") for k in range(3)]
        node_vector = [sem(f"node_vector{k}") for k in range(3)]
        node_root = [sem(f"node_root{k}") for k in range(3)]
        node_out = [sem(f"node_out{k}") for k in range(3)]
        edge_vector = [sem(f"edge_vector{l}") for l in range(2)]
        edge_tensor = [sem(f"edge_tensor{l}") for l in range(2)]
        edge_in = [sem(f"edge_in{l}") for l in range(2)]
        edge_out = [sem(f"edge_out{l}") for l in range(2)]
        sums_zeroed = sem("sums_zeroed")

        NODE_V = [5, 7, 8]
        EDGE_V, EDGE_T = 13, 6

        def wait_apart(eng, semaphore, value):
            eng.wait_ge(semaphore, value)
            eng.sem_inc(waited, 1)

        def sp_general(sp):
            def node_step(k, base, n):
                table = x if k == 0 else sums_dram
                sp.dma_start(g_rows[:, 0, :], table[bass.ds(base, P), :]).then_inc(node_in[k], 16)
                if k == 2:
                    sp.dma_start(g_x[:, :], x[bass.ds(base, P), :]).then_inc(node_in[k], 16)
                wait_apart(sp, node_vector[k], NODE_V[k] * n + NODE_V[k])
                target = (h_dram[0], h_dram[1], out)[k]
                sp.dma_start(target[bass.ds(base, P), :], g_node[:, 4, :]).then_inc(node_out[k], 16)
                wait_apart(sp, node_out[k], 16 * n + 16)

            sp.wait_ge(setup_done, 3)
            for k in range(3):
                if k:
                    sp.dma_start(sums_dram.rearrange("(t p) d -> p t d", p=P),
                                 g_zero[:, :].unsqueeze(1).to_broadcast([P, SUM_TILES, D])).then_inc(sums_zeroed, 16)
                    sp.wait_ge(edge_out[k - 1], 16 * EDGE_TILES)
                with sp.Fori(0, NODE_TILES - 1) as n:
                    node_step(k, n * P, n)
                node_step(k, LAST, NODE_TILES - 1)

        def pool_general(pool):
            for l in range(2):
                pool.wait_ge(node_out[l], 16 * NODE_TILES)
                pool.wait_ge(sums_zeroed, 16 * (l + 1))
                with pool.Fori(0, EDGE_TILES) as t:
                    wait_apart(pool, edge_vector[l], EDGE_V * t + 7)
                    for c, table in enumerate((h_dram[l][0:N, :], h_dram[l][0:N, :], sums_dram)):
                        pool.indirect_dma_start(g_rows[:, c, :], None, table,
                                                bass.IndirectOffsetOnAxis(g_idx[:, c:c + 1], 0)).then_inc(edge_in[l], 16)
                    wait_apart(pool, edge_vector[l], EDGE_V * t + EDGE_V)
                    pool.indirect_dma_start(sums_dram, bass.IndirectOffsetOnAxis(g_idx[:, 2:3], 0),
                                            g_msg[:, 1, :], None).then_inc(edge_out[l], 16)
                    wait_apart(pool, edge_out[l], 16 * t + 16)

        def vector_general(dve):
            def node_steps(k, n, steps):
                def step(ins):
                    steps[0] += 1
                    ins.then_inc(node_vector[k], 1)
                    wait_apart(dve, node_vector[k], NODE_V[k] * n + steps[0])

                dve.wait_ge(node_in[k], (16 if k < 2 else 32) * n + (16 if k < 2 else 32))
                step(nc.vector.bn_stats(g_stats[:, :], g_rows[:, 0, :]))
                step(nc.vector.bn_aggr(g_mean[:, :], g_stats[:, :]))
                dve.wait_ge(node_root[k], n + 1)
                step(nc.vector.reciprocal(g_root[:, 1:2], g_root[:, 0:1]))
                if k == 0:
                    step(nc.vector.tensor_scalar(g_node[:, 0, :], g_rows[:, 0, :], g_mean[:, 0:1], 0.0,
                                                 ALU.subtract, ALU.max))
                    step(nc.vector.tensor_scalar(g_node[:, 4, :], g_node[:, 0, :], g_root[:, 1:2], None, ALU.mult))
                    return
                step(nc.vector.tensor_scalar(g_node[:, 0, :], g_rows[:, 0, :], g_mean[:, 0:1], g_root[:, 1:2],
                                             ALU.subtract, ALU.mult))
                step(nc.vector.tensor_tensor(g_node[:, 1, :], g_node[:, 0, :], vecs[:, k - 1, 2, :], ALU.mult))
                step(nc.vector.tensor_tensor(g_node[:, 2, :], g_node[:, 1, :], vecs[:, k - 1, 3, :], ALU.add))
                last = g_node[:, 4, :] if k == 1 else g_node[:, 3, :]
                step(nc.vector.scalar_tensor_tensor(last, g_node[:, 2, :], SLOPE, g_node[:, 2, :], ALU.mult, ALU.max))
                if k == 2:
                    step(nc.vector.tensor_tensor(g_node[:, 4, :], g_node[:, 3, :], g_x[:, :], ALU.add))

            def edge_steps(l, t):
                count = [0]

                def step(ins):
                    count[0] += 1
                    ins.then_inc(edge_vector[l], 1)
                    wait_apart(dve, edge_vector[l], EDGE_V * t + count[0])

                dst_col = dst_cols[:, bass.ds(t, 1)]
                step(nc.vector.tensor_copy(g_key[:, :], dst_col.to_broadcast([P, P])))
                step(nc.vector.tensor_copy(g_idx[:, 1:2], src_cols[:, bass.ds(t, 1)]))
                step(nc.vector.tensor_scalar(g_idx[:, 0:1], dst_col, float(N - 1), None, ALU.min))
                dve.wait_ge(edge_tensor[l], EDGE_T * t + 1)
                step(nc.vector.tensor_scalar(g_same[:, 0, :], psum[0][:, 0, :], dst_col, None, ALU.is_equal))
                step(nc.vector.tensor_tensor_reduce(g_same[:, 1, :], g_same[:, 0, :], earlier[:, :], 1.0, 0.0,
                                                    ALU.mult, ALU.max, g_col[:, 0:1]))
                step(nc.vector.tensor_scalar(g_col[:, 1:2], lane_dump[:, :], dst_col, g_col[:, 0:1],
                                             ALU.subtract, ALU.mult))
                step(nc.vector.tensor_scalar(g_idx[:, 2:3], dst_col, g_col[:, 1:2], None, ALU.add))
                dve.wait_ge(edge_tensor[l], EDGE_T * t + 2)
                step(nc.vector.tensor_copy(g_hT[:, :, :], psum[1][:, 0:2, :]))
                dve.wait_ge(edge_tensor[l], EDGE_T * t + 3)
                step(nc.vector.tensor_tensor(g_hid[:, 0, :], psum[2][:, 0, :], vecs[:, l, 0, :], ALU.add))
                step(nc.vector.scalar_tensor_tensor(g_hid[:, 1, :], g_hid[:, 0, :], SLOPE, g_hid[:, 0, :],
                                                    ALU.mult, ALU.max))
                dve.wait_ge(edge_tensor[l], EDGE_T * t + 4)
                step(nc.vector.tensor_copy(g_hidT[:, :], psum[3][:, 0, :]))
                dve.wait_ge(edge_tensor[l], EDGE_T * t + 5)
                step(nc.vector.tensor_tensor(g_msg[:, 0, :], psum[4][:, 0, :], vecs[:, l, 1, :], ALU.add))
                dve.wait_ge(edge_tensor[l], EDGE_T * t + 6)
                step(nc.vector.tensor_tensor(g_msg[:, 1, :], psum[5][:, 0, :], g_rows[:, 2, :], ALU.add))
                assert count[0] == EDGE_V

            for k in range(3):
                if k:
                    with dve.Fori(0, EDGE_TILES) as t:
                        edge_steps(k - 1, t)
                        dve.wait_ge(edge_out[k - 1], 16 * t + 16)
                with dve.Fori(0, NODE_TILES) as n:
                    node_steps(k, n, [0])
                    dve.wait_ge(node_out[k], 16 * n + 16)

        def tensor_general(pe):
            for l in range(2):
                with pe.Fori(0, EDGE_TILES) as t:
                    def after(dve_steps):
                        pe.wait_ge(edge_vector[l], EDGE_V * t + dve_steps)
                    after(1)
                    nc.tensor.transpose(psum[0][:, 0, :], g_key[:, :], ident[:, :]).then_inc(edge_tensor[l], 1)
                    pe.wait_ge(edge_in[l], 48 * t + 48)
                    for c in range(2):
                        last = nc.tensor.transpose(psum[1][:, c, :], g_rows[:, c, :], ident[:, :])
                    last.then_inc(edge_tensor[l], 1)
                    after(8)
                    nc.tensor.matmul(psum[2][:, 0, :], g_hT[:, 0, :], w1d[l][:, :], start=True, stop=False)
                    nc.tensor.matmul(psum[2][:, 0, :], g_hT[:, 1, :], w1[l][:, 1, :], start=False,
                                     stop=True).then_inc(edge_tensor[l], 1)
                    after(10)
                    nc.tensor.transpose(psum[3][:, 0, :], g_hid[:, 1, :], ident[:, :]).then_inc(edge_tensor[l], 1)
                    after(11)
                    nc.tensor.matmul(psum[4][:, 0, :], g_hidT[:, :], w2[l][:, :], start=True,
                                     stop=True).then_inc(edge_tensor[l], 1)
                    after(12)
                    nc.tensor.matmul(psum[5][:, 0, :], g_same[:, 0, :], g_msg[:, 0, :], start=True,
                                     stop=True).then_inc(edge_tensor[l], 1)

        block = ctx.enter_context(nc.Block())

        @block.sync
        def _(sp):
            sp.wait_ge(masks_made, 4)
            full, rest = E // ROW, E % ROW
            for c, a in enumerate((src, dst)):
                sp.dma_start(edge_rows[0:full, c, :],
                             a[0:full * ROW].rearrange("(p c) -> p c", c=ROW)).then_inc(edges_loaded, 16)
                sp.dma_start(edge_rows[full:PAIRS, c, 0:rest],
                             a[full * ROW:E].rearrange("(p c) -> p c", p=1)).then_inc(edges_loaded, 16)
            for l in range(2):
                W1, b1, W2, b2, g, b = weights[l]
                sp.dma_start(w1[l][:, :, :], W1.rearrange("(a p) n -> p a n", a=2)).then_inc(weights_loaded, 16)
                sp.dma_start(w2[l][:, :], W2).then_inc(weights_loaded, 16)
                for c, v in enumerate((b1, b2, g, b)):
                    sp.dma_start(vec_row[0:1, l, c, :], v.rearrange("(a d) -> a d", a=1)).then_inc(weights_loaded, 16)
            sp_general(sp)

        @block.gpsimd
        def _(pool):
            pool.memset(edge_rows[:, 0, :], 0).then_inc(masks_made, 1)
            pool.iota(edge_rows[:, 1, :].rearrange("p (a c) -> p a c", a=2), pattern=[[0, 2], [1, P]],
                      base=NPAD, channel_multiplier=0).then_inc(masks_made, 1)
            pool.iota(lane_dump[:, :], pattern=[[0, 1]], base=NPAD, channel_multiplier=1,
                      allow_small_or_imprecise_dtypes=True).then_inc(blanks_made, 1)
            pool.memset(ident[:, :], 0.0).then_inc(blanks_made, 1)
            pool.memset(earlier[:, :], 1.0).then_inc(blanks_made, 1)
            pool.wait_ge(blanks_made, 3)
            pool.affine_select(out=ident[:, :], in_=ident[:, :], compare_op=ALU.not_equal, fill=1.0, base=0,
                               pattern=[[-1, P]], channel_multiplier=1).then_inc(masks_made, 1)
            pool.affine_select(out=earlier[:, :], in_=earlier[:, :], compare_op=ALU.is_gt, fill=0.0, base=0,
                               pattern=[[-1, P]], channel_multiplier=1).then_inc(masks_made, 1)
            pool_general(pool)

        @block.scalar
        def _(act):
            act.wait_ge(setup_done, 3)
            for k in range(3):
                with act.Fori(0, NODE_TILES) as n:
                    act.wait_ge(node_vector[k], NODE_V[k] * n + 2)
                    nc.scalar.activation(g_root[:, 0:1], g_mean[:, 1:2], ACT.Sqrt,
                                         bias=eps_col[:, 0:1]).then_inc(node_root[k], 1)

        @block.vector
        def _(dve):
            nc.vector.memset(eps_col[:, :], EPS).then_inc(consts_set, 1)
            nc.vector.memset(g_zero[:, :], 0.0).then_inc(consts_set, 1)
            nc.vector.memset(ones_row[:, :], 1.0).then_inc(consts_set, 1)
            dve.wait_ge(edges_loaded, 64)
            nc.vector.tensor_copy(edge_rows_f[:, :, :], edge_rows[:, :, :]).then_inc(edges_cast, 1)
            dve.wait_ge(turned, 1)
            for k in range(2):
                nc.vector.tensor_copy(src_cols[:, k:EDGE_TILES:2], psum[k][:, 0, 0:PAIRS]).then_inc(cols_made, 1)
                nc.vector.tensor_copy(dst_cols[:, k:EDGE_TILES:2], psum[k][:, 1, 0:PAIRS]).then_inc(cols_made, 1)
            dve.wait_ge(weights_loaded, 16 * 12)
            dve.wait_ge(turned, 2)
            for l in range(2):
                nc.vector.tensor_tensor(w1d[l][:, :], w1[l][:, 0, :], w1[l][:, 1, :], ALU.subtract).then_inc(cols_made, 1)
                nc.vector.tensor_copy(vecs[:, l, :, :], psum[2 + l][:, :, :]).then_inc(cols_made, 1)
            dve.wait_ge(consts_set, 3)
            dve.wait_ge(cols_made, 8)
            nc.vector.memset(g_root[:, :], 0.0).then_inc(setup_done, 3)
            dve.wait_ge(setup_done, 3)
            vector_general(dve)

        @block.tensor
        def _(pe):
            pe.wait_ge(masks_made, 4)
            pe.wait_ge(edges_cast, 1)
            for k in range(2):
                for c in range(2):
                    last = nc.tensor.transpose(psum[k][:, c, 0:PAIRS], edge_rows_f[:, c, k * P:k * P + P],
                                               ident[0:PAIRS, 0:PAIRS])
            last.then_inc(turned, 1)
            pe.wait_ge(weights_loaded, 16 * 12)
            pe.wait_ge(consts_set, 3)
            for l in range(2):
                last = nc.tensor.matmul(psum[2 + l][:, :, :], ones_row[0:1, :], vec_row[0:1, l, :, :],
                                        start=True, stop=True)
            last.then_inc(turned, 1)
            tensor_general(pe)


def kernel(x, src, dst, L0_gnn_W1_0, L0_gnn_b1_0, L0_gnn_W2_0, L0_gnn_b2_0, L0_gnn_ln_g0, L0_gnn_ln_b0,
           L0_gnn_W1_1, L0_gnn_b1_1, L0_gnn_W2_1, L0_gnn_b2_1, L0_gnn_ln_g1, L0_gnn_ln_b1):
    import numpy as _np
    import concourse.bacc as _bacc
    from concourse.bass_utils import run_bass_kernel_spmd as _run

    given = dict(x=x, src=src, dst=dst, W1_0=L0_gnn_W1_0, b1_0=L0_gnn_b1_0, W2_0=L0_gnn_W2_0, b2_0=L0_gnn_b2_0,
                 g_0=L0_gnn_ln_g0, b_0=L0_gnn_ln_b0, W1_1=L0_gnn_W1_1, b1_1=L0_gnn_b1_1, W2_1=L0_gnn_W2_1,
                 b2_1=L0_gnn_b2_1, g_1=L0_gnn_ln_g1, b_1=L0_gnn_ln_b1)
    nc = _bacc.Bacc("TRN2", target_bir_lowering=False, num_devices=1)
    arrays, aps = {}, {}
    for name, a in given.items():
        a = _np.ascontiguousarray(a)
        arrays[f"in_{name}"] = a
        aps[name] = nc.dram_tensor(f"in_{name}", a.shape, mybir.dt.from_np(a.dtype), kind="ExternalInput").ap()
    out = nc.dram_tensor("out", list(aps["x"].shape), F32, kind="ExternalOutput").ap()
    weights = [tuple(aps[f"{v}_{l}"] for v in ("W1", "b1", "W2", "b2", "g", "b")) for l in range(2)]
    build(nc, aps["x"], aps["src"], aps["dst"], weights, out)
    r = _run(nc, [arrays], core_ids=[0])
    return r.results[0]["out"]
```

```python
from contextlib import ExitStack

import concourse.bass as bass
from concourse import mybir

F32 = mybir.dt.float32
I32 = mybir.dt.int32
ALU = mybir.AluOpType
ACT = mybir.ActivationFunctionType
AX = mybir.AxisListType

P = 128
EPS = 1e-5
SLOPE = 0.01
RING = 4
LAG = 7
FIRST = -3


class Group:

    def __init__(self, i, c):
        self.i, self.c = i, c
        self.static = isinstance(i, int)
        self.slot, self.half = c % RING, c % 2
        self.active = not self.static or 0 <= c < Group.COUNT
        self.last = self.static and c == Group.COUNT - 1

    def __add__(self, k):
        return Group(self.i, self.c + k)

    def __sub__(self, k):
        return Group(self.i, self.c - k)

    @property
    def n(self):
        return self.c if self.static else self.i * RING + self.c

    @property
    def q(self):
        return self.c // RING if self.static else self.i + self.c // RING

    @property
    def n2(self):
        return self.c // 2 if self.static else self.i * 2 + self.c // 2


def build(nc, x, src, dst, weights, out):
    N, D = x.shape
    E = src.shape[0]
    NODE_TILES = -(-N // P)
    ROW = 2 * P
    PAIRS = -(-E // ROW)
    EDGE_TILES = 2 * PAIRS
    NPAD = -(-N // (4 * P)) * 4 * P
    SUM_TILES = NPAD // P + 1
    GROUPS = NPAD // (4 * P)
    assert GROUPS == PAIRS and GROUPS % 2 == 0
    Group.COUNT = GROUPS
    LAST_STEP = GROUPS + LAG + 4
    LOOP_FROM = LAG + 7
    LOOPS = (GROUPS - 3 - LOOP_FROM) // RING
    LAST_LOADS = N // P - (GROUPS - 1) * 4 + 1
    SIDE = 20
    STARTS = SIDE * SIDE
    AHEAD = 448
    PAD = 98304.0
    LAST = N - P

    h_dram = [nc.dram_tensor(f"h{l}_rows", [NPAD, D], F32, kind="Internal").ap() for l in range(2)]
    sums_dram = nc.dram_tensor("sums_rows", [SUM_TILES * P, D], F32, kind="Internal").ap()

    b_dram = nc.dram_tensor("b_rows", [(PAIRS + 1) * ROW, D + 1], F32, kind="Internal").ap()
    starts_dram = nc.dram_tensor("starts", [STARTS], I32, kind="Internal").ap()

    with ExitStack() as ctx:
        def sb(name, shape, dt=F32):
            return ctx.enter_context(nc.sbuf_tensor(name, shape, dt))

        def sem(name):
            return ctx.enter_context(nc.semaphore(name))

        ident = sb("ident", [P, P])
        ones_row = sb("ones_row", [1, P])
        eps_col = sb("eps_col", [P, 1])
        edge_rows = sb("edge_rows", [PAIRS, 2, ROW], I32)
        edge_rows_f = sb("edge_rows_f", [PAIRS, 2, ROW])
        next_rows = sb("next_rows", [PAIRS, ROW])
        next_in = sb("next_in", [PAIRS, ROW], I32)
        dst_cols = sb("dst_cols", [P, EDGE_TILES])
        src_cols = sb("src_cols", [P, EDGE_TILES], I32)
        w1 = [sb(f"w1_{l}", [P, 2, D]) for l in range(2)]
        w1d = [sb(f"w1d_{l}", [P, D]) for l in range(2)]
        w2 = [sb(f"w2_{l}", [P, D]) for l in range(2)]
        vec_row = sb("vec_row", [1, 2, 4, D])
        vecs = sb("vecs", [P, 2, 4, D])
        psum = [ctx.enter_context(nc.psum_tensor(f"psum{i}", [P, 4, P], F32)) for i in range(8)]

        blanks_made = sem("blanks_made")
        masks_made = sem("masks_made")
        consts_set = sem("consts_set")
        edges_loaded = sem("edges_loaded")
        weights_loaded = sem("weights_loaded")
        edges_cast = sem("edges_cast")
        cols_made = sem("cols_made")
        downs_made = sem("downs_made")
        waited = sem("waited")
        hand = sem("hand")
        counted = sem("counted")
        starts_out = sem("starts_out")
        starts_in = sem("starts_in")
        flag_made = sem("flag_made")
        b_padded = sem("b_padded")
        blank_set = sem("blank_set")

        BF16 = mybir.dt.bfloat16
        limits = sb("limits", [P, 2, SIDE + 1])
        below_q = sb("below_q", [P, EDGE_TILES, SIDE + 1], BF16)
        in_q = sb("in_q", [P, EDGE_TILES, SIDE], BF16)
        below_r = sb("below_r", [P, EDGE_TILES, SIDE], BF16)
        q_left = sb("q_left", [P, 2, EDGE_TILES])
        q_sums = sb("q_sums", [P, SIDE])
        q_col = sb("q_col", [SIDE, 1])
        start_sq = sb("start_sq", [SIDE, SIDE])
        start_sqi = sb("start_sqi", [SIDE, SIDE], I32)
        start_f = sb("start_f", [1, STARTS])
        excess = sb("excess", [1, 2, NODE_TILES])
        even_rate = sb("even_rate", [1, NODE_TILES])
        down = sb("down", [PAIRS, ROW])
        downs = sb("downs", [PAIRS, 1])
        bad = sb("bad", [1, 8])
        flag = sb("flag", [1, 1], I32)
        b_blank = sb("b_blank", [P, 2, D + 1])
        turned = sem("turned")
        setup_done = sem("setup_done")

        earlier = sb("earlier", [P, P])
        lane_dump = sb("lane_dump", [P, 1])
        g_rows = sb("g_rows", [P, 3, D])
        g_hT = sb("g_hT", [P, 2, P])
        g_hid = sb("g_hid", [P, 2, P])
        g_hidT = sb("g_hidT", [P, P])
        g_msg = sb("g_msg", [P, 2, D])
        g_key = sb("g_key", [P, P])
        g_same = sb("g_same", [P, 2, P])
        g_col = sb("g_col", [P, 2])
        g_idx = sb("g_idx", [P, 3], I32)
        g_node = sb("g_node", [P, 5, D])
        g_x = sb("g_x", [P, D])
        g_stats = sb("g_stats", [P, 6])
        g_mean = sb("g_mean", [P, 2])
        g_root = sb("g_root", [P, 2])
        g_zero = sb("g_zero", [P, D])

        node_in = [sem(f"node_in{k}") for k in range(3)]
        node_vector = [sem(f"node_vector{k}") for k in range(3)]
        node_root = [sem(f"node_root{k}") for k in range(3)]
        node_out = [sem(f"node_out{k}") for k in range(3)]
        edge_vector = [sem(f"edge_vector{l}") for l in range(2)]
        edge_tensor = [sem(f"edge_tensor{l}") for l in range(2)]
        edge_in = [sem(f"edge_in{l}") for l in range(2)]
        edge_out = [sem(f"edge_out{l}") for l in range(2)]
        sums_zeroed = sem("sums_zeroed")

        CONSTS = 7
        FLAG = 4
        row_mean = sb("row_mean", [P, 2])
        b2c = sb("b2c", [P, 2, D])
        MASKS = 10
        NODE_V = [5, 7, 8]
        EDGE_V, EDGE_T = 13, 6


        ones_col = sb("ones_col", [P, 1])
        node_iota = sb("node_iota", [P, 4, P])
        group_neg = sb("group_neg", [P, GROUPS])
        w2c = [sb(f"w2c_{l}", [P, D]) for l in range(2)]
        start_row = sb("start_row", [1, STARTS], I32)
        w_idx = sb("w_idx", [P, RING, 2], I32)
        w_xj = sb("w_xj", [P, RING, 2, D])
        w_x = sb("w_x", [P, RING, 4, D])
        w_win = sb("w_win", [P, RING, 4, D + 1])
        w_xf = sb("w_xf", [P, RING, 4, D])
        w_hj = sb("w_hj", [P, 2, 2, D])
        w_h = sb("w_h", [P, 2, 4, D])
        w_hjT = sb("w_hjT", [P, 2, P])
        w_b = sb("w_b", [P, 2, 2, D + 1])
        w_rel = sb("w_rel", [P, 4])
        w_oh = sb("w_oh", [P, RING, 4, P])
        w_ohT = sb("w_ohT", [P, 2, 4, P])
        w_xiT = sb("w_xiT", [P, 4 * P])
        w_z = sb("w_z", [P, 2, 4, D])
        w_hid = sb("w_hid", [P, 2, 4, D])
        w_agT = sb("w_agT", [P, 4 * P])
        w_sq = sb("w_sq", [P, 4, D])
        w_ssq = sb("w_ssq", [P, 2, 4])
        w_scaled = sb("w_scaled", [P, 2, 4, D])
        w_fin = sb("w_fin", [P, 2, 4, D])
        w_leak = sb("w_leak", [P, 2, 4, D])
        w_pos = sb("w_pos", [P, 2, 4, D])
        w_out = sb("w_out", [P, 2, 4, D])
        w_stats = sb("w_stats", [P, 6, 6])
        w_mean = sb("w_mean", [P, 6, 2])
        w_var = sb("w_var", [P, 10])
        w_root = sb("w_root", [P, 10])
        w_inv = sb("w_inv", [P, 10])
        w_shift = sb("w_shift", [P, 6])
        p_ohT, p_y, p_h = psum[0], (psum[4], psum[7]), psum[2]
        p_xiT = psum[1][:, :, :].rearrange("p a b -> p (a b)")
        p_agT = psum[3][:, :, :].rearrange("p a b -> p (a b)")
        p_hjT, p_b = psum[5][:, 0:2, :], psum[6][:, 0:2, :]

        def per_layer(name):
            return [sem(f"{name}{l}") for l in range(2)]

        xj_in = [[sem(f"xj_in{l}_{k}") for k in range(RING)] for l in range(2)]
        x_in = [[sem(f"x_in{l}_{k}") for k in range(RING)] for l in range(2)]
        win_in = [[sem(f"win_in{l}_{k}") for k in range(RING)] for l in range(2)]
        xf_in = [sem(f"xf_in{k}") for k in range(RING)]
        b_out = [[sem(f"b_out{l}_{k}") for k in range(2)] for l in range(2)]
        stored = [[sem(f"stored{l}_{k}") for k in range(2)] for l in range(2)]
        index_made = per_layer("index_made")
        stats_made, means_made, var_made = per_layer("stats_made"), per_layer("means_made"), per_layer("var_made")
        rooted, inv_made, shift_made = per_layer("rooted"), per_layer("inv_made"), per_layer("shift_made")
        hj_made, h_made = per_layer("hj_made"), per_layer("h_made")
        rel_made, oh_made = per_layer("rel_made"), per_layer("oh_made")
        oh_turned, ohT_copied = per_layer("oh_turned"), per_layer("ohT_copied")
        x_selected, xiT_copied = per_layer("x_selected"), per_layer("xiT_copied")
        h_summed, z_made, hid_made = per_layer("h_summed"), per_layer("z_made"), per_layer("hid_made")
        aggregated, agT_copied, y_summed = per_layer("aggregated"), per_layer("agT_copied"), per_layer("y_summed")
        squared, scaled = per_layer("squared"), per_layer("scaled")
        biased, sloped, leaked, maxed = per_layer("biased"), per_layer("sloped"), per_layer("leaked"), sem("maxed")
        hj_turned, hjT_copied = per_layer("hj_turned"), per_layer("hjT_copied")
        b_summed, b_made = per_layer("b_summed"), per_layer("b_made")

        def root_active(l, s):
            return not s.static or (-1 if l == 0 else LAG + 3) <= s.n <= GROUPS + LAG + 2

        def root_count(l, s):
            return s.n + 1 - (-1 if l == 0 else LAG + 3)

        def wait_apart(eng, semaphore, value):
            eng.wait_ge(semaphore, value)
            eng.sem_inc(waited, 1)

        def sp_general(sp):
            def node_step(k, base, n):
                table = x if k == 0 else sums_dram
                sp.dma_start(g_rows[:, 0, :], table[bass.ds(base, P), :]).then_inc(node_in[k], 16)
                if k == 2:
                    sp.dma_start(g_x[:, :], x[bass.ds(base, P), :]).then_inc(node_in[k], 16)
                wait_apart(sp, node_vector[k], NODE_V[k] * n + NODE_V[k])
                target = (h_dram[0], h_dram[1], out)[k]
                sp.dma_start(target[bass.ds(base, P), :], g_node[:, 4, :]).then_inc(node_out[k], 16)
                wait_apart(sp, node_out[k], 16 * n + 16)

            sp.wait_ge(setup_done, 3)
            for k in range(3):
                if k:
                    sp.dma_start(sums_dram.rearrange("(t p) d -> p t d", p=P),
                                 g_zero[:, :].unsqueeze(1).to_broadcast([P, SUM_TILES, D])).then_inc(sums_zeroed, 16)
                    sp.wait_ge(edge_out[k - 1], 16 * EDGE_TILES)
                with sp.Fori(0, NODE_TILES - 1) as n:
                    node_step(k, n * P, n)
                node_step(k, LAST, NODE_TILES - 1)

        def pool_general(pool):
            for l in range(2):
                pool.wait_ge(node_out[l], 16 * NODE_TILES)
                pool.wait_ge(sums_zeroed, 16 * (l + 1))
                with pool.Fori(0, EDGE_TILES) as t:
                    wait_apart(pool, edge_vector[l], EDGE_V * t + 7)
                    for c, table in enumerate((h_dram[l][0:N, :], h_dram[l][0:N, :], sums_dram)):
                        pool.indirect_dma_start(g_rows[:, c, :], None, table,
                                                bass.IndirectOffsetOnAxis(g_idx[:, c:c + 1], 0)).then_inc(edge_in[l], 16)
                    wait_apart(pool, edge_vector[l], EDGE_V * t + EDGE_V)
                    pool.indirect_dma_start(sums_dram, bass.IndirectOffsetOnAxis(g_idx[:, 2:3], 0),
                                            g_msg[:, 1, :], None).then_inc(edge_out[l], 16)
                    wait_apart(pool, edge_out[l], 16 * t + 16)

        def scalar_general(act):
            for k in range(3):
                with act.Fori(0, NODE_TILES) as n:
                    act.wait_ge(node_vector[k], NODE_V[k] * n + 2)
                    nc.scalar.activation(g_root[:, 0:1], g_mean[:, 1:2], ACT.Sqrt,
                                         bias=eps_col[:, 0:1]).then_inc(node_root[k], 1)

        def vector_general(dve):
            def node_steps(k, n, steps):
                def step(ins):
                    steps[0] += 1
                    ins.then_inc(node_vector[k], 1)
                    wait_apart(dve, node_vector[k], NODE_V[k] * n + steps[0])

                dve.wait_ge(node_in[k], (16 if k < 2 else 32) * n + (16 if k < 2 else 32))
                step(nc.vector.bn_stats(g_stats[:, :], g_rows[:, 0, :]))
                step(nc.vector.bn_aggr(g_mean[:, :], g_stats[:, :]))
                dve.wait_ge(node_root[k], n + 1)
                step(nc.vector.reciprocal(g_root[:, 1:2], g_root[:, 0:1]))
                if k == 0:
                    step(nc.vector.tensor_scalar(g_node[:, 0, :], g_rows[:, 0, :], g_mean[:, 0:1], 0.0,
                                                 ALU.subtract, ALU.max))
                    step(nc.vector.tensor_scalar(g_node[:, 4, :], g_node[:, 0, :], g_root[:, 1:2], None, ALU.mult))
                    return
                step(nc.vector.tensor_scalar(g_node[:, 0, :], g_rows[:, 0, :], g_mean[:, 0:1], g_root[:, 1:2],
                                             ALU.subtract, ALU.mult))
                step(nc.vector.tensor_tensor(g_node[:, 1, :], g_node[:, 0, :], vecs[:, k - 1, 2, :], ALU.mult))
                step(nc.vector.tensor_tensor(g_node[:, 2, :], g_node[:, 1, :], vecs[:, k - 1, 3, :], ALU.add))
                last = g_node[:, 4, :] if k == 1 else g_node[:, 3, :]
                step(nc.vector.scalar_tensor_tensor(last, g_node[:, 2, :], SLOPE, g_node[:, 2, :], ALU.mult, ALU.max))
                if k == 2:
                    step(nc.vector.tensor_tensor(g_node[:, 4, :], g_node[:, 3, :], g_x[:, :], ALU.add))

            def edge_steps(l, t):
                count = [0]

                def step(ins):
                    count[0] += 1
                    ins.then_inc(edge_vector[l], 1)
                    wait_apart(dve, edge_vector[l], EDGE_V * t + count[0])

                dst_col = dst_cols[:, bass.ds(t, 1)]
                step(nc.vector.tensor_copy(g_key[:, :], dst_col.to_broadcast([P, P])))
                step(nc.vector.tensor_copy(g_idx[:, 1:2], src_cols[:, bass.ds(t, 1)]))
                step(nc.vector.tensor_scalar(g_idx[:, 0:1], dst_col, float(N - 1), None, ALU.min))
                dve.wait_ge(edge_tensor[l], EDGE_T * t + 1)
                step(nc.vector.tensor_scalar(g_same[:, 0, :], psum[0][:, 0, :], dst_col, None, ALU.is_equal))
                step(nc.vector.tensor_tensor_reduce(g_same[:, 1, :], g_same[:, 0, :], earlier[:, :], 1.0, 0.0,
                                                    ALU.mult, ALU.max, g_col[:, 0:1]))
                step(nc.vector.tensor_scalar(g_col[:, 1:2], lane_dump[:, :], dst_col, g_col[:, 0:1],
                                             ALU.subtract, ALU.mult))
                step(nc.vector.tensor_scalar(g_idx[:, 2:3], dst_col, g_col[:, 1:2], None, ALU.add))
                dve.wait_ge(edge_tensor[l], EDGE_T * t + 2)
                step(nc.vector.tensor_copy(g_hT[:, :, :], psum[1][:, 0:2, :]))
                dve.wait_ge(edge_tensor[l], EDGE_T * t + 3)
                step(nc.vector.tensor_tensor(g_hid[:, 0, :], psum[2][:, 0, :], vecs[:, l, 0, :], ALU.add))
                step(nc.vector.scalar_tensor_tensor(g_hid[:, 1, :], g_hid[:, 0, :], SLOPE, g_hid[:, 0, :],
                                                    ALU.mult, ALU.max))
                dve.wait_ge(edge_tensor[l], EDGE_T * t + 4)
                step(nc.vector.tensor_copy(g_hidT[:, :], psum[3][:, 0, :]))
                dve.wait_ge(edge_tensor[l], EDGE_T * t + 5)
                step(nc.vector.tensor_tensor(g_msg[:, 0, :], psum[4][:, 0, :], vecs[:, l, 1, :], ALU.add))
                dve.wait_ge(edge_tensor[l], EDGE_T * t + 6)
                step(nc.vector.tensor_tensor(g_msg[:, 1, :], psum[5][:, 0, :], g_rows[:, 2, :], ALU.add))
                assert count[0] == EDGE_V

            for k in range(3):
                if k:
                    with dve.Fori(0, EDGE_TILES) as t:
                        edge_steps(k - 1, t)
                        dve.wait_ge(edge_out[k - 1], 16 * t + 16)
                with dve.Fori(0, NODE_TILES) as n:
                    node_steps(k, n, [0])
                    dve.wait_ge(node_out[k], 16 * n + 16)

        def tensor_general(pe):
            for l in range(2):
                with pe.Fori(0, EDGE_TILES) as t:
                    def after(dve_steps):
                        pe.wait_ge(edge_vector[l], EDGE_V * t + dve_steps)
                    after(1)
                    nc.tensor.transpose(psum[0][:, 0, :], g_key[:, :], ident[:, :]).then_inc(edge_tensor[l], 1)
                    pe.wait_ge(edge_in[l], 48 * t + 48)
                    for c in range(2):
                        last = nc.tensor.transpose(psum[1][:, c, :], g_rows[:, c, :], ident[:, :])
                    last.then_inc(edge_tensor[l], 1)
                    after(8)
                    nc.tensor.matmul(psum[2][:, 0, :], g_hT[:, 0, :], w1d[l][:, :], start=True, stop=False)
                    nc.tensor.matmul(psum[2][:, 0, :], g_hT[:, 1, :], w1[l][:, 1, :], start=False,
                                     stop=True).then_inc(edge_tensor[l], 1)
                    after(10)
                    nc.tensor.transpose(psum[3][:, 0, :], g_hid[:, 1, :], ident[:, :]).then_inc(edge_tensor[l], 1)
                    after(11)
                    nc.tensor.matmul(psum[4][:, 0, :], g_hidT[:, :], w2[l][:, :], start=True,
                                     stop=True).then_inc(edge_tensor[l], 1)
                    after(12)
                    nc.tensor.matmul(psum[5][:, 0, :], g_same[:, 0, :], g_msg[:, 0, :], start=True,
                                     stop=True).then_inc(edge_tensor[l], 1)


        def need(eng, semaphore, count):
            if not isinstance(count, int) or count > 0:
                eng.wait_ge(semaphore, count)

        def need_apart(eng, semaphore, count):
            if not isinstance(count, int):
                wait_apart(eng, semaphore, count)
            elif count > 0:
                eng.wait_ge(semaphore, count)

        def run_steps(eng, step):
            for s in range(FIRST, LOOP_FROM):
                step(Group(0, s))
            with eng.Fori(0, LOOPS) as i:
                for u in range(RING):
                    step(Group(i, LOOP_FROM + u))
            for s in range(LOOP_FROM + RING * LOOPS, LAST_STEP + 1):
                step(Group(0, s))

        def sp_windowed(sp, l):
            nodes = x if l == 0 else h_dram[1]
            target = h_dram[1] if l == 0 else out
            starts = [sp.alloc_register(f"start{l}_{j}") for j in range(4)]

            def load_nodes(table, to, g, signal):
                if table is x and g.last:
                    whole = (N - g.n * 4 * P) // P
                    for j in range(whole):
                        sp.dma_start(to[:, g.slot, j, :], x[g.n * 4 * P + j * P:g.n * 4 * P + (j + 1) * P, :]).then_inc(signal[g.slot], 16)
                    sp.dma_start(to[0:N % P, g.slot, whole, :], x[N - N % P:N, :]).then_inc(signal[g.slot], 16)
                else:
                    sp.dma_start(to[:, g.slot, :, :],
                                 table[bass.ds(g.n * (4 * P), 4 * P), :].rearrange("(j p) d -> p j d", p=P)).then_inc(signal[g.slot], 16)

            def step(s):
                a = s - LAG
                g = a + 3
                if g.active:
                    need_apart(sp, h_made[l] if l == 0 else x_selected[l], g.n - 3)
                    load_nodes(nodes, w_x, g, x_in[l])
                w = a + 3
                if w.active:
                    sp.load(starts, start_row[0:1, bass.ds(w.n * 4, 4)])
                    need_apart(sp, (h_summed if l == 0 else z_made)[l], w.n - 3)
                    p = w + 2 if not w.static or w.n + 2 < PAIRS else Group(0, PAIRS - 1)
                    need_apart(sp, b_out[l][0], (p.n2 + 1) * 16)
                    need_apart(sp, b_out[l][1], ((p + 1).n2) * 16)
                    for j in range(4):
                        at = sp.snap(starts[j], min_val=0, max_val=E)
                        sp.dma_start(w_win[:, w.slot, j, :], b_dram[bass.ds(at, P), :]).then_inc(win_in[l][w.slot], 16)
                if l == 1:
                    v = a - 3
                    if v.active:
                        need_apart(sp, leaked[l], v.n - 3)
                        load_nodes(x, w_xf, v, xf_in)
                o = a - 5
                if o.active:
                    need_apart(sp, leaked[l], o.n + 1)
                    if l == 1 and o.last:
                        whole = (N - o.n * 4 * P) // P
                        sp.dma_start(out[o.n * 4 * P:o.n * 4 * P + whole * P, :].rearrange("(j p) d -> p j d", p=P),
                                     w_out[:, o.half, 0:whole, :]).then_inc(stored[l][o.half], 16)
                        sp.dma_start(out[N - N % P:N, :], w_out[0:N % P, o.half, whole, :]).then_inc(stored[l][o.half], 16)
                    else:
                        sp.dma_start(target[bass.ds(o.n * (4 * P), 4 * P), :].rearrange("(j p) d -> p j d", p=P),
                                     w_out[:, o.half, :, :]).then_inc(stored[l][o.half], 16)
                e = s - 1
                if e.active:
                    need_apart(sp, b_made[l], e.n + 1)
                    sp.dma_start(b_dram[bass.ds(e.n * ROW, ROW), :].rearrange("(k p) d -> p k d", p=P),
                                 w_b[:, e.half, :, :]).then_inc(b_out[l][e.half], 16)

            run_steps(sp, step)
            for half in range(2):
                sp.wait_ge(stored[l][half], 16 * (GROUPS // 2) + (16 if l == 1 and half == (GROUPS - 1) % 2 else 0))
                sp.wait_ge(b_out[l][half], 16 * (PAIRS // 2))

        def pool_windowed(pool, l):
            table = x if l == 0 else h_dram[1][0:N, :]
            if l == 1:
                for half in range(2):
                    pool.wait_ge(stored[0][half], 16 * (GROUPS // 2))

            b_all = vecs[:, l, 3, :].unsqueeze(1).to_broadcast([P, 4, D])

            def step(s):
                e, a = s + 3, s - LAG
                if e.active:
                    if not e.static or e.n >= RING:
                        need_apart(pool, xj_in[l][e.slot], e.q * 32)
                    pool.tensor_copy(w_idx[:, e.slot, :], src_cols[:, bass.ds(e.n * 2, 2)]).then_inc(index_made[l], 1)
                    need_apart(pool, hj_made[l] if l == 0 else hj_turned[l], e.n - 3)
                    need_apart(pool, index_made[l], e.n + 1)
                    for k in range(2):
                        pool.indirect_dma_start(w_xj[:, e.slot, k, :], None, table,
                                                bass.IndirectOffsetOnAxis(w_idx[:, e.slot, k:k + 1], 0)).then_inc(xj_in[l][e.slot], 16)
                o, f = a - 4, a - 3
                if o.active:
                    need_apart(pool, sloped[l], o.n + 1)
                    if not o.static or o.n >= 2:
                        need_apart(pool, stored[l][o.half], o.n2 * 16)
                    last = pool.tensor_tensor(w_out[:, o.half, :, :], w_pos[:, o.half, :, :], w_leak[:, o.half, :, :], ALU.add)
                    if l == 1:
                        last.then_inc(maxed, 1)
                        need_apart(pool, maxed, o.n + 1)
                        need_apart(pool, xf_in[o.slot], (o.q + 1) * 16 + (LAST_LOADS * 16 - 16 if o.last else 0))
                        last = pool.tensor_tensor(w_out[:, o.half, :, :], w_out[:, o.half, :, :], w_xf[:, o.slot, :, :], ALU.add)
                    last.then_inc(leaked[l], 1)
                if l == 0 and f.active:
                    need_apart(pool, scaled[l], f.n + 1)
                    pool.tensor_tensor(w_fin[:, f.half, :, :], w_scaled[:, f.half, :, :], b_all, ALU.add).then_inc(biased[l], 1)

            run_steps(pool, step)

        def scalar_windowed(act, l):
            selected = ACT.Relu if l == 0 else ACT.Copy

            def step(s):
                e, a = s, s - LAG
                t, g, q, o = a + 1, a - 1, a - 2, a - 4
                if t.active:
                    act.wait_ge(oh_turned[l], t.n + 1)
                    need(act, x_selected[l], t.n - 1)
                    nc.scalar.activation(w_ohT[:, t.half, :, :], p_ohT[:, :, :], ACT.Copy).then_inc(ohT_copied[l], 1)
                if a.active:
                    act.wait_ge(x_selected[l], a.n + 1)
                    need(act, h_summed[l], a.n)
                    nc.scalar.activation(w_xiT[:, :], p_xiT[:, :], selected).then_inc(xiT_copied[l], 1)
                if root_active(l, s):
                    act.wait_ge(var_made[l], root_count(l, s))
                    cols = slice(0, 10) if l == 0 else slice(6, 10)
                    nc.scalar.activation(w_root[:, cols], w_var[:, cols], ACT.Sqrt).then_inc(rooted[l], 1)
                if g.active:
                    act.wait_ge(aggregated[l], g.n + 1)
                    need(act, y_summed[l], g.n)
                    nc.scalar.activation(w_agT[:, :], p_agT[:, :], ACT.Copy).then_inc(agT_copied[l], 1)
                if e.active:
                    act.wait_ge(hj_turned[l], e.n + 1)
                    need(act, b_summed[l], e.n)
                    nc.scalar.activation(w_hjT[:, :, :], p_hjT, selected).then_inc(hjT_copied[l], 1)
                if q.active:
                    act.wait_ge(y_summed[l], q.n + 1)
                    for j in range(4):
                        last = nc.scalar.activation(w_sq[:, j, :], p_y[q.half][:, j, :], ACT.Square,
                                                    accum_out=w_ssq[:, q.half, j:j + 1])
                    last.then_inc(squared[l], 1)
                if l == 0 and a.active:
                    act.wait_ge(h_summed[l], a.n + 1)
                    need(act, hid_made[l], a.n - 1)
                    nc.scalar.activation(w_z[:, a.half, :, :], p_h[:, :, :], ACT.Copy, scale=SLOPE).then_inc(z_made[l], 1)
                if l == 0 and t.active:
                    act.wait_ge(shift_made[l], root_count(l, s))
                    need(act, x_selected[l], t.n - 1)
                    for j in range(4):
                        last = nc.scalar.activation(w_h[:, t.half, j, :], w_x[:, t.slot, j, :], ACT.Identity,
                                                    bias=w_shift[:, 2 + j:3 + j], scale=w_inv[:, 2 + j:3 + j])
                    last.then_inc(h_made[l], 1)
                if o.active:
                    act.wait_ge(biased[l], o.n + 1)
                    need(act, leaked[l], o.n - 1)
                    nc.scalar.activation(w_leak[:, o.half, :, :], w_fin[:, o.half, :, :], ACT.Copy, scale=SLOPE)
                    nc.scalar.activation(w_pos[:, o.half, :, :], w_fin[:, o.half, :, :], ACT.Relu,
                                         scale=1.0 - SLOPE).then_inc(sloped[l], 1)

            run_steps(act, step)

        def vector_windowed(dve, l):
            b1_all, g_all, b_all = (vecs[:, l, c, :] for c in (0, 2, 3))

            def step(s):
                e, a = s, s - LAG
                e1, a1, a2, f = s + 1, a + 1, a + 2, a - 3
                norm_pair, norm_nodes = l == 0 and e1.active, l == 0 and a1.active
                if norm_pair:
                    dve.wait_ge(xj_in[l][e1.slot], (e1.q + 1) * 32)
                    for k in range(2):
                        last = nc.vector.bn_stats(w_stats[:, k, :], w_xj[:, e1.slot, k, :])
                if norm_nodes:
                    dve.wait_ge(x_in[l][a1.slot], (a1.q + 1) * 16 + (LAST_LOADS * 16 - 16 if a1.last else 0))
                    for j in range(4):
                        last = nc.vector.bn_stats(w_stats[:, 2 + j, :], w_x[:, a1.slot, j, :])
                if norm_pair or norm_nodes:
                    last.then_inc(stats_made[l], 1)
                    dve.wait_ge(stats_made[l], root_count(l, s))
                if f.active:
                    dve.wait_ge(squared[l], f.n + 1)
                    last = nc.vector.tensor_scalar(w_var[:, 6:10], w_ssq[:, f.half, :], 1.0 / D, EPS, ALU.mult, ALU.add)
                if norm_pair or norm_nodes:
                    lo, hi = (0 if norm_pair else 2), (6 if norm_nodes else 2)
                    for k in range(lo, hi):
                        last = nc.vector.bn_aggr(w_mean[:, k, :], w_stats[:, k, :])
                    last.then_inc(means_made[l], 1)
                    dve.wait_ge(means_made[l], root_count(l, s))
                    last = nc.vector.tensor_scalar(w_var[:, lo:hi], w_mean[:, lo:hi, 1], EPS, None, ALU.add)
                if root_active(l, s):
                    last.then_inc(var_made[l], 1)
                if a2.active:
                    dve.wait_ge(win_in[l][a2.slot], (a2.q + 1) * 64)
                    need(dve, oh_made[l], a2.n)
                    nc.vector.tensor_scalar(w_rel[:, :], w_win[:, a2.slot, :, D], group_neg[:, bass.ds(a2.n, 1)], None,
                                            ALU.add).then_inc(rel_made[l], 1)
                    need(dve, y_summed[l], a2.n - 3)
                    dve.wait_ge(rel_made[l], a2.n + 1)
                    nc.vector.tensor_tensor(w_oh[:, a2.slot, :, :], node_iota[:, :, :],
                                            w_rel[:, :].unsqueeze(2).to_broadcast([P, 4, P]), ALU.is_equal).then_inc(oh_made[l], 1)
                if root_active(l, s):
                    dve.wait_ge(rooted[l], root_count(l, s))
                    if norm_nodes:
                        need(dve, h_made[l], a1.n)
                    cols = slice(0, 10) if l == 0 else slice(6, 10)
                    nc.vector.reciprocal(w_inv[:, cols], w_root[:, cols]).then_inc(inv_made[l], 1)
                    dve.wait_ge(inv_made[l], root_count(l, s))
                if norm_pair or norm_nodes:
                    nc.vector.scalar_tensor_tensor(w_shift[:, :], w_mean[:, :, 0], -1.0, w_inv[:, 0:6], ALU.mult,
                                                   ALU.mult).then_inc(shift_made[l], 1)
                    dve.wait_ge(shift_made[l], root_count(l, s))
                if norm_pair:
                    need(dve, hj_turned[l], e1.n - 1)
                    for k in range(2):
                        last = nc.vector.tensor_scalar(w_hj[:, e1.half, k, :], w_xj[:, e1.slot, k, :], w_inv[:, k:k + 1],
                                                       w_shift[:, k:k + 1], ALU.mult, ALU.add)
                    last.then_inc(hj_made[l], 1)
                if f.active:
                    need(dve, biased[l], f.n - 1)
                    for j in range(4):
                        last = nc.vector.scalar_tensor_tensor(w_scaled[:, f.half, j, :], p_y[f.half][:, j, :], w_inv[:, 6 + j:7 + j],
                                                              g_all, ALU.mult, ALU.mult)
                    last.then_inc(scaled[l], 1)
                if l == 0 and a.active:
                    dve.wait_ge(z_made[l], a.n + 1)
                    need(dve, aggregated[l], a.n - 1)
                    nc.vector.tensor_tensor(w_hid[:, a.half, :, :], p_h[:, :, :], w_z[:, a.half, :, :], ALU.max).then_inc(hid_made[l], 1)
                if l == 1 and a.active:
                    dve.wait_ge(h_summed[l], a.n + 1)
                    nc.vector.tensor_tensor(w_z[:, a.half, :, :], p_h[:, :, :], w_win[:, a.slot, :, 0:D], ALU.add).then_inc(z_made[l], 1)
                if l == 1 and f.active:
                    dve.wait_ge(scaled[l], f.n + 1)
                    need(dve, sloped[l], f.n - 1)
                    nc.vector.tensor_tensor(w_fin[:, f.half, :, :], w_scaled[:, f.half, :, :],
                                            b_all.unsqueeze(1).to_broadcast([P, 4, D]), ALU.add).then_inc(biased[l], 1)
                if l == 1 and a.active:
                    dve.wait_ge(z_made[l], a.n + 1)
                    need(dve, aggregated[l], a.n - 1)
                    nc.vector.scalar_tensor_tensor(w_hid[:, a.half, :, :], w_z[:, a.half, :, :], SLOPE, w_z[:, a.half, :, :],
                                                   ALU.mult, ALU.max).then_inc(hid_made[l], 1)
                if e.active:
                    dve.wait_ge(b_summed[l], e.n + 1)
                    if not e.static or e.n >= 2:
                        dve.wait_ge(b_out[l][e.half], e.n2 * 16)
                    nc.vector.tensor_tensor(w_b[:, e.half, :, 0:D], p_b, b1_all.unsqueeze(1).to_broadcast([P, 2, D]), ALU.add)
                    nc.vector.tensor_copy(w_b[:, e.half, :, D], dst_cols[:, bass.ds(e.n * 2, 2)]).then_inc(b_made[l], 1)

            run_steps(dve, step)

        def tensor_windowed(pe, l):
            w1b = w1[l][:, 1, :]

            def step(s):
                e, a = s, s - LAG
                t, g = a + 1, a - 1
                if t.active:
                    pe.wait_ge(oh_made[l], t.n + 1)
                    need(pe, ohT_copied[l], t.n)
                    for j in range(4):
                        last = nc.tensor.transpose(p_ohT[:, j, :], w_oh[:, t.slot, j, :], ident[:, :])
                    last.then_inc(oh_turned[l], 1)
                if a.active:
                    pe.wait_ge(ohT_copied[l], a.n + 1)
                    need(pe, xiT_copied[l], a.n)
                    if l == 0:
                        pe.wait_ge(h_made[l], a.n + 1)
                    else:
                        pe.wait_ge(x_in[l][a.slot], (a.q + 1) * 16)
                    for j in range(4):
                        rows = w_h[:, a.half, j, :] if l == 0 else w_x[:, a.slot, j, :]
                        last = nc.tensor.matmul(p_xiT[:, j * P:(j + 1) * P], rows, w_ohT[:, a.half, j, :], start=True, stop=True)
                    last.then_inc(x_selected[l], 1)
                if g.active:
                    pe.wait_ge(hid_made[l], g.n + 1)
                    need(pe, agT_copied[l], g.n)
                    for j in range(4):
                        last = nc.tensor.matmul(p_agT[:, j * P:(j + 1) * P], w_hid[:, g.half, j, :], w_oh[:, g.slot, j, :],
                                                start=True, stop=True)
                    last.then_inc(aggregated[l], 1)
                if e.active:
                    if l == 0:
                        pe.wait_ge(hj_made[l], e.n + 1)
                    else:
                        pe.wait_ge(xj_in[l][e.slot], (e.q + 1) * 32)
                    need(pe, hjT_copied[l], e.n)
                    for k in range(2):
                        rows = w_hj[:, e.half, k, :] if l == 0 else w_xj[:, e.slot, k, :]
                        last = nc.tensor.transpose(p_hjT[:, k, :], rows, ident[:, :])
                    last.then_inc(hj_turned[l], 1)
                if a.active:
                    pe.wait_ge(xiT_copied[l], a.n + 1)
                    need(pe, (hid_made if l == 0 else z_made)[l], a.n)
                    for j in range(4):
                        last = nc.tensor.matmul(p_h[:, j, :], w_xiT[:, j * P:(j + 1) * P], w1d[l][:, :], start=True, stop=l == 1)
                        if l == 0:
                            last = nc.tensor.matmul(p_h[:, j, :], ident[:, :], w_win[:, a.slot, j, 0:D], start=False, stop=True)
                    last.then_inc(h_summed[l], 1)
                if e.active:
                    pe.wait_ge(hjT_copied[l], e.n + 1)
                    need(pe, b_made[l], e.n)
                    for k in range(2):
                        last = nc.tensor.matmul(p_b[:, k, :], w_hjT[:, k, :], w1b, start=True, stop=True)
                    last.then_inc(b_summed[l], 1)
                if g.active:
                    pe.wait_ge(agT_copied[l], g.n + 1)
                    need(pe, scaled[l], g.n - 1)
                    for j in range(4):
                        nc.tensor.matmul(p_y[g.half][:, j, :], w_agT[:, j * P:(j + 1) * P], w2c[l][:, :], start=True, stop=False)
                        last = nc.tensor.matmul(p_y[g.half][:, j, :], w_oh[:, g.slot, j, :], b2c[:, l, :], start=False, stop=True)
                    last.then_inc(y_summed[l], 1)

            run_steps(pe, step)

        block = ctx.enter_context(nc.Block())

        @block.sync
        def _(sp):
            sp.wait_ge(masks_made, MASKS)
            full, rest = E // ROW, E % ROW
            for c, a in enumerate((src, dst)):
                sp.dma_start(edge_rows[0:full, c, :],
                             a[0:full * ROW].rearrange("(p c) -> p c", c=ROW)).then_inc(edges_loaded, 16)
                sp.dma_start(edge_rows[full:PAIRS, c, 0:rest],
                             a[full * ROW:E].rearrange("(p c) -> p c", p=1)).then_inc(edges_loaded, 16)
            sp.dma_start(next_in[0:full, :], dst[1:full * ROW + 1].rearrange("(p c) -> p c", c=ROW)).then_inc(edges_loaded, 16)
            sp.dma_start(next_in[full:PAIRS, 0:rest - 1],
                         dst[full * ROW + 1:E].rearrange("(p c) -> p c", p=1)).then_inc(edges_loaded, 16)
            for l in range(2):
                W1, b1, W2, b2, g, b = weights[l]
                sp.dma_start(w1[l][:, :, :], W1.rearrange("(a p) n -> p a n", a=2)).then_inc(weights_loaded, 16)
                sp.dma_start(w2[l][:, :], W2).then_inc(weights_loaded, 16)
                for c, v in enumerate((b1, b2, g, b)):
                    sp.dma_start(vec_row[0:1, l, c, :], v.rearrange("(a d) -> a d", a=1)).then_inc(weights_loaded, 16)
            sp.wait_ge(masks_made, MASKS)
            sp.wait_ge(blank_set, 2)
            sp.dma_start(b_dram[PAIRS * ROW:, :].rearrange("(k p) d -> p k d", p=P), b_blank[:, :, :]).then_inc(b_padded, 16)
            sp.wait_ge(counted, 2)
            sp.dma_start(starts_dram.rearrange("(q r) -> q r", q=SIDE), start_sqi[:, :]).then_inc(starts_out, 16)
            sp.wait_ge(starts_out, 16)
            sp.dma_start(start_row[:, :], starts_dram.rearrange("(a n) -> a n", a=1)).then_inc(starts_in, 16)
            sp.wait_ge(b_padded, 16)
            sp.wait_ge(flag_made, 1)
            ok = sp.value_load(flag[0:1, 0:1], min_val=0, max_val=1)
            with sp.If(ok == 1):
                for l in range(2):
                    sp_windowed(sp, l)
            with sp.Else():
                sp_general(sp)

        @block.gpsimd
        def _(pool):
            pool.memset(edge_rows[:, 0, :], 0).then_inc(masks_made, 1)
            pool.iota(edge_rows[:, 1, :].rearrange("p (a c) -> p a c", a=2), pattern=[[0, 2], [1, P]],
                      base=NPAD, channel_multiplier=0).then_inc(masks_made, 1)
            pool.iota(lane_dump[:, :], pattern=[[0, 1]], base=NPAD, channel_multiplier=1,
                      allow_small_or_imprecise_dtypes=True).then_inc(blanks_made, 1)
            pool.memset(ident[:, :], 0.0).then_inc(blanks_made, 1)
            pool.memset(earlier[:, :], 1.0).then_inc(blanks_made, 1)
            pool.wait_ge(blanks_made, 3)
            pool.affine_select(out=ident[:, :], in_=ident[:, :], compare_op=ALU.not_equal, fill=1.0, base=0,
                               pattern=[[-1, P]], channel_multiplier=1).then_inc(masks_made, 1)
            pool.affine_select(out=earlier[:, :], in_=earlier[:, :], compare_op=ALU.is_gt, fill=0.0, base=0,
                               pattern=[[-1, P]], channel_multiplier=1).then_inc(masks_made, 1)
            pool.memset(next_in[:, :], int(PAD)).then_inc(masks_made, 1)
            pool.iota(node_iota[:, :, :], pattern=[[P, 4], [1, P]], base=0, channel_multiplier=0,
                      allow_small_or_imprecise_dtypes=True).then_inc(masks_made, 1)
            pool.iota(group_neg[:, :], pattern=[[-4 * P, GROUPS]], base=0, channel_multiplier=0,
                      allow_small_or_imprecise_dtypes=True).then_inc(masks_made, 1)
            pool.iota(limits[:, 0, :], pattern=[[SIDE * P, SIDE + 1]], base=0, channel_multiplier=0,
                      allow_small_or_imprecise_dtypes=True).then_inc(masks_made, 1)
            pool.iota(limits[:, 1, :], pattern=[[P, SIDE + 1]], base=0, channel_multiplier=0,
                      allow_small_or_imprecise_dtypes=True).then_inc(masks_made, 1)
            pool.iota(even_rate[:, :], pattern=[[P * E // N, NODE_TILES]], base=0, channel_multiplier=0,
                      allow_small_or_imprecise_dtypes=True).then_inc(masks_made, 1)
            pool.memset(b_blank[:, :, 0:D], 0.0).then_inc(blank_set, 1)
            pool.memset(b_blank[:, :, D:D + 1], -1.0).then_inc(blank_set, 1)
            pool.wait_ge(flag_made, 1)
            ok = pool.value_load(flag[0:1, 0:1], min_val=0, max_val=1)
            with pool.If(ok == 1):
                for l in range(2):
                    pool_windowed(pool, l)
            with pool.Else():
                pool_general(pool)

        @block.scalar
        def _(act):
            act.wait_ge(flag_made, 1)
            ok = act.value_load(flag[0:1, 0:1], min_val=0, max_val=1)
            with act.If(ok == 1):
                for l in range(2):
                    scalar_windowed(act, l)
            with act.Else():
                scalar_general(act)

        @block.vector
        def _(dve):
            nc.vector.memset(eps_col[:, :], EPS).then_inc(consts_set, 1)
            nc.vector.memset(g_zero[:, :], 0.0).then_inc(consts_set, 1)
            nc.vector.memset(ones_row[:, :], 1.0).then_inc(consts_set, 1)
            nc.vector.memset(ones_col[:, :], 1.0).then_inc(consts_set, 1)
            nc.vector.memset(w_var[:, :], 1.0).then_inc(consts_set, 1)
            nc.vector.memset(w_mean[:, :, :], 0.0).then_inc(consts_set, 1)
            nc.vector.memset(w_x[:, :, :, :], 0.0).then_inc(consts_set, 1)

            hands = [0]

            def step(ins):
                hands[0] += 1
                ins.then_inc(hand, 1)
                dve.wait_ge(hand, hands[0])

            dve.wait_ge(edges_loaded, 96)
            nc.vector.tensor_copy(edge_rows_f[:, :, :], edge_rows[:, :, :]).then_inc(edges_cast, 1)
            step(nc.vector.tensor_copy(next_rows[:, :], next_in[:, :]))
            dve.wait_ge(edges_cast, 1)
            step(nc.vector.tensor_tensor(down[:, :], edge_rows_f[:, 1, :], next_rows[:, :], ALU.is_gt))
            nc.vector.tensor_reduce(downs[:, :], down[:, :], AX.X, ALU.add).then_inc(downs_made, 1)
            dve.wait_ge(turned, 1)
            for k in range(2):
                nc.vector.tensor_copy(src_cols[:, k:EDGE_TILES:2], psum[k][:, 0, 0:PAIRS]).then_inc(cols_made, 1)
                nc.vector.tensor_copy(dst_cols[:, k:EDGE_TILES:2], psum[k][:, 1, 0:PAIRS]).then_inc(cols_made, 1)
            dve.wait_ge(cols_made, 4)
            dve.wait_ge(masks_made, MASKS)

            def per_limit(cols, limit, width):
                return (cols.unsqueeze(2).to_broadcast([P, EDGE_TILES, width]),
                        limit.unsqueeze(1).to_broadcast([P, EDGE_TILES, width]))

            step(nc.vector.tensor_tensor(below_q[:, :, :], *per_limit(dst_cols[:, :], limits[:, 0, :], SIDE + 1), ALU.is_lt))
            step(nc.vector.tensor_tensor(in_q[:, :, :], below_q[:, :, 1:SIDE + 1], below_q[:, :, 0:SIDE], ALU.subtract))
            step(nc.vector.tensor_reduce(q_left[:, 0, :], below_q[:, :, 0:SIDE], AX.X, ALU.add))
            step(nc.vector.tensor_scalar(q_left[:, 0, :], q_left[:, 0, :], float(SIDE * P), float(-(SIDE - 1) * SIDE * P),
                                         ALU.mult, ALU.add))
            step(nc.vector.tensor_tensor(q_left[:, 1, :], q_left[:, 0, :], dst_cols[:, :], ALU.add))
            step(nc.vector.tensor_tensor(below_r[:, :, :], *per_limit(q_left[:, 1, :], limits[:, 1, 0:SIDE], SIDE), ALU.is_lt))
            nc.vector.tensor_reduce(q_sums[:, :], below_q[:, :, 0:SIDE].rearrange("p t q -> p q t"), AX.X,
                                    ALU.add).then_inc(counted, 1)
            dve.wait_ge(turned, 2)
            step(nc.vector.tensor_copy(q_col[:, :], psum[4][0:SIDE, 0, 0:1]))
            step(nc.vector.tensor_scalar(start_sq[:, :], psum[7][0:SIDE, 0, 0:SIDE], q_col[:, 0:1], None, ALU.add))
            nc.vector.tensor_copy(start_sqi[:, :], start_sq[:, :]).then_inc(counted, 1)

            dve.wait_ge(weights_loaded, 16 * 12)
            dve.wait_ge(turned, 3)
            for l in range(2):
                nc.vector.tensor_tensor(w1d[l][:, :], w1[l][:, 0, :], w1[l][:, 1, :], ALU.subtract).then_inc(cols_made, 1)
                step(nc.vector.tensor_copy(vecs[:, l, :, :], psum[2 + l][:, :, :]))
                for whole, less in ((w2[l][:, :], w2c[l][:, :]), (vecs[:, l, 1, :], b2c[:, l, :])):
                    step(nc.vector.tensor_reduce(row_mean[:, 0:1], whole, AX.X, ALU.add))
                    step(nc.vector.tensor_scalar(row_mean[:, 1:2], row_mean[:, 0:1], 1.0 / D, None, ALU.mult))
                    step(nc.vector.tensor_scalar(less, whole, row_mean[:, 1:2], None, ALU.subtract))
            dve.wait_ge(starts_in, 16)
            step(nc.vector.tensor_copy(start_f[:, :], start_row[:, :]))
            step(nc.vector.tensor_tensor(excess[:, 0, :], start_f[:, 1:NODE_TILES + 1], start_f[:, 0:NODE_TILES], ALU.subtract))
            step(nc.vector.tensor_tensor(excess[:, 1, :], start_f[:, 0:NODE_TILES], even_rate[:, :], ALU.subtract))
            step(nc.vector.tensor_reduce(bad[:, 0:2], excess[:, :, :], AX.X, ALU.max))
            step(nc.vector.tensor_scalar(bad[:, 2:3], bad[:, 0:1], float(P), None, ALU.is_le))
            step(nc.vector.tensor_scalar(bad[:, 3:4], bad[:, 1:2], float(AHEAD), bad[:, 2:3], ALU.is_le, ALU.mult))
            step(nc.vector.tensor_scalar(bad[:, 4:5], psum[5][0:1, 0, 0:1], 0.0, bad[:, 3:4], ALU.is_equal, ALU.mult))
            step(nc.vector.tensor_copy(flag[:, :], bad[:, FLAG:FLAG + 1]))
            dve.wait_ge(consts_set, CONSTS)
            dve.wait_ge(cols_made, 6)
            nc.vector.memset(g_root[:, :], 0.0).then_inc(setup_done, 3)
            dve.wait_ge(setup_done, 3)
            nc.vector.memset(bad[:, 6:7], 0.0).then_inc(flag_made, 1)
            dve.wait_ge(flag_made, 1)
            ok = dve.value_load(flag[0:1, 0:1], min_val=0, max_val=1)
            with dve.If(ok == 1):
                for l in range(2):
                    vector_windowed(dve, l)
            with dve.Else():
                vector_general(dve)

        @block.tensor
        def _(pe):
            pe.wait_ge(masks_made, MASKS)
            pe.wait_ge(edges_cast, 1)
            for k in range(2):
                for c in range(2):
                    last = nc.tensor.transpose(psum[k][:, c, 0:PAIRS], edge_rows_f[:, c, k * P:k * P + P],
                                               ident[0:PAIRS, 0:PAIRS])
            last.then_inc(turned, 1)
            pe.wait_ge(consts_set, CONSTS)
            pe.wait_ge(counted, 1)
            for t in range(EDGE_TILES):
                nc.tensor.matmul(psum[7][0:SIDE, 0, 0:SIDE], in_q[:, t, :], below_r[:, t, :], start=(t == 0),
                                 stop=(t == EDGE_TILES - 1))
            nc.tensor.matmul(psum[4][0:SIDE, 0, 0:1], q_sums[:, :], ones_col[:, :], start=True, stop=True).then_inc(turned, 1)
            pe.wait_ge(downs_made, 1)
            nc.tensor.matmul(psum[5][0:1, 0, 0:1], downs[:, :], ones_col[0:PAIRS, :], start=True, stop=True)
            pe.wait_ge(weights_loaded, 16 * 12)
            for l in range(2):
                last = nc.tensor.matmul(psum[2 + l][:, :, :], ones_row[0:1, :], vec_row[0:1, l, :, :],
                                        start=True, stop=True)
            last.then_inc(turned, 1)
            pe.wait_ge(flag_made, 1)
            ok = pe.value_load(flag[0:1, 0:1], min_val=0, max_val=1)
            with pe.If(ok == 1):
                for l in range(2):
                    tensor_windowed(pe, l)
            with pe.Else():
                tensor_general(pe)



def kernel(x, src, dst, L0_gnn_W1_0, L0_gnn_b1_0, L0_gnn_W2_0, L0_gnn_b2_0, L0_gnn_ln_g0, L0_gnn_ln_b0,
           L0_gnn_W1_1, L0_gnn_b1_1, L0_gnn_W2_1, L0_gnn_b2_1, L0_gnn_ln_g1, L0_gnn_ln_b1):
    import numpy as _np
    import concourse.bacc as _bacc
    from concourse.bass_utils import run_bass_kernel_spmd as _run

    given = dict(x=x, src=src, dst=dst, W1_0=L0_gnn_W1_0, b1_0=L0_gnn_b1_0, W2_0=L0_gnn_W2_0, b2_0=L0_gnn_b2_0,
                 g_0=L0_gnn_ln_g0, b_0=L0_gnn_ln_b0, W1_1=L0_gnn_W1_1, b1_1=L0_gnn_b1_1, W2_1=L0_gnn_W2_1,
                 b2_1=L0_gnn_b2_1, g_1=L0_gnn_ln_g1, b_1=L0_gnn_ln_b1)
    nc = _bacc.Bacc("TRN2", target_bir_lowering=False, num_devices=1)
    arrays, aps = {}, {}
    for name, a in given.items():
        a = _np.ascontiguousarray(a)
        arrays[f"in_{name}"] = a
        aps[name] = nc.dram_tensor(f"in_{name}", a.shape, mybir.dt.from_np(a.dtype), kind="ExternalInput").ap()
    out = nc.dram_tensor("out", list(aps["x"].shape), F32, kind="ExternalOutput").ap()
    weights = [tuple(aps[f"{v}_{l}"] for v in ("W1", "b1", "W2", "b2", "g", "b")) for l in range(2)]
    build(nc, aps["x"], aps["src"], aps["dst"], weights, out)
    r = _run(nc, [arrays], core_ids=[0])
    return r.results[0]["out"]
```

```python
from contextlib import ExitStack

import concourse.bass as bass
from concourse import mybir

F32 = mybir.dt.float32
I32 = mybir.dt.int32
ALU = mybir.AluOpType
ACT = mybir.ActivationFunctionType
AX = mybir.AxisListType

P = 128
EPS = 1e-5
SLOPE = 0.01
RING = 4
W = 112
PE_ADDS = 2
LAG = 8
FIRST = -3
EARLY = LAG - 3


class Group:

    def __init__(self, i, c):
        self.i, self.c = i, c
        self.static = isinstance(i, int)
        self.slot, self.half = c % RING, c % 2
        self.active = not self.static or 0 <= c < Group.COUNT
        self.last = self.static and c == Group.COUNT - 1

    def __add__(self, k):
        return Group(self.i, self.c + k)

    def __sub__(self, k):
        return Group(self.i, self.c - k)

    @property
    def n(self):
        return self.c if self.static else self.i * RING + self.c

    @property
    def before(self):
        return min(self.n, Group.COUNT) if self.static else self.n

    @property
    def q(self):
        return self.c // RING if self.static else self.i + self.c // RING

    @property
    def n2(self):
        return self.c // 2 if self.static else self.i * 2 + self.c // 2


def build(nc, x, src, dst, weights, out):
    N, D = x.shape
    E = src.shape[0]
    NODE_TILES = -(-N // P)
    ROW = 2 * P
    PAIRS = -(-E // ROW)
    EDGE_TILES = 2 * PAIRS
    NPAD = -(-N // (4 * P)) * 4 * P
    SUM_TILES = NPAD // P + 1
    GROUPS = NPAD // (4 * P)
    assert GROUPS == PAIRS and GROUPS % 2 == 0
    Group.COUNT = GROUPS
    LAST_STEP = GROUPS + LAG + 5
    LOOP_FROM = LAG + 8
    LOOPS = (GROUPS - 3 - LOOP_FROM) // RING
    LAST_LOADS = N // P - (GROUPS - 1) * 4 + 1
    COLS = 16
    LINES = NODE_TILES // COLS + 1
    STARTS = LINES * COLS
    PB, CB = P.bit_length() - 1, COLS.bit_length() - 1
    AHEAD = 448
    PAD = 98304.0
    LAST = N - P

    h_dram = [nc.dram_tensor(f"h{l}_rows", [NPAD, D], F32, kind="Internal").ap() for l in range(2)]
    sums_dram = nc.dram_tensor("sums_rows", [SUM_TILES * P, D], F32, kind="Internal").ap()

    b_dram = nc.dram_tensor("b_rows", [(PAIRS + 1) * ROW, D + 1], F32, kind="Internal").ap()
    starts_dram = nc.dram_tensor("starts", [STARTS], I32, kind="Internal").ap()

    with ExitStack() as ctx:
        def sb(name, shape, dt=F32):
            return ctx.enter_context(nc.sbuf_tensor(name, shape, dt))

        def sem(name):
            return ctx.enter_context(nc.semaphore(name))

        ident = sb("ident", [P, P])
        ones_row = sb("ones_row", [1, P])
        eps_col = sb("eps_col", [P, 1])
        edge_rows = sb("edge_rows", [PAIRS, 2, ROW], I32)
        edge_rows_f = sb("edge_rows_f", [PAIRS, 2, ROW])
        next_rows = sb("next_rows", [PAIRS, ROW])
        next_in = sb("next_in", [PAIRS, ROW], I32)
        dst_cols = sb("dst_cols", [P, EDGE_TILES])
        src_cols = sb("src_cols", [P, EDGE_TILES], I32)
        w1 = [sb(f"w1_{l}", [P, 2, D]) for l in range(2)]
        w1d = [sb(f"w1d_{l}", [P, D]) for l in range(2)]
        w2 = [sb(f"w2_{l}", [P, D]) for l in range(2)]
        vec_row = sb("vec_row", [1, 2, 4, D])
        vecs = sb("vecs", [P, 2, 4, D])
        psum = [ctx.enter_context(nc.psum_tensor(f"psum{i}", [P, 4, P], F32)) for i in range(8)]

        blanks_made = sem("blanks_made")
        masks_made = sem("masks_made")
        consts_set = sem("consts_set")
        edges_loaded = sem("edges_loaded")
        weights_loaded = sem("weights_loaded")
        edges_cast = sem("edges_cast")
        cols_made = sem("cols_made")
        downs_made = sem("downs_made")
        waited = sem("waited")
        hand = sem("hand")
        counted = sem("counted")
        starts_out = sem("starts_out")
        starts_in = sem("starts_in")
        flag_made = sem("flag_made")
        b_padded = sem("b_padded")
        blank_set = sem("blank_set")
        table_made = sem("table_made")
        parts_made = sem("parts_made")

        BF16 = mybir.dt.bfloat16
        number = sb("number", [P, LINES], BF16)
        dst_int = sb("dst_int", [P, 3, EDGE_TILES], I32)
        dst_part = sb("dst_part", [P, 2, EDGE_TILES], BF16)
        in_line = sb("in_line", [P, EDGE_TILES, LINES], BF16)
        below_col = sb("below_col", [P, EDGE_TILES, COLS + 1], BF16)
        line_counts = sb("line_counts", [LINES, 1])
        lower_lines = sb("lower_lines", [LINES, LINES])
        start_table = sb("start_table", [LINES, COLS], I32)
        start_f = sb("start_f", [1, STARTS])
        excess = sb("excess", [1, 2, NODE_TILES])
        even_rate = sb("even_rate", [1, NODE_TILES])
        down = sb("down", [PAIRS, ROW])
        downs = sb("downs", [PAIRS, 1])
        bad = sb("bad", [1, 8])
        flag = sb("flag", [1, 1], I32)
        b_blank = sb("b_blank", [P, 2, D + 1])
        turned = sem("turned")
        setup_done = sem("setup_done")

        earlier = sb("earlier", [P, P])
        lane_dump = sb("lane_dump", [P, 1])
        g_rows = sb("g_rows", [P, 3, D])
        g_hT = sb("g_hT", [P, 2, P])
        g_hid = sb("g_hid", [P, 2, P])
        g_hidT = sb("g_hidT", [P, P])
        g_msg = sb("g_msg", [P, 2, D])
        g_key = sb("g_key", [P, P])
        g_same = sb("g_same", [P, 2, P])
        g_col = sb("g_col", [P, 2])
        g_idx = sb("g_idx", [P, 3], I32)
        g_node = sb("g_node", [P, 5, D])
        g_x = sb("g_x", [P, D])
        g_stats = sb("g_stats", [P, 6])
        g_mean = sb("g_mean", [P, 2])
        g_root = sb("g_root", [P, 2])
        g_zero = sb("g_zero", [P, D])

        node_in = [sem(f"node_in{k}") for k in range(3)]
        node_vector = [sem(f"node_vector{k}") for k in range(3)]
        node_root = [sem(f"node_root{k}") for k in range(3)]
        node_out = [sem(f"node_out{k}") for k in range(3)]
        edge_vector = [sem(f"edge_vector{l}") for l in range(2)]
        edge_tensor = [sem(f"edge_tensor{l}") for l in range(2)]
        edge_in = [sem(f"edge_in{l}") for l in range(2)]
        edge_out = [sem(f"edge_out{l}") for l in range(2)]
        sums_zeroed = sem("sums_zeroed")

        CONSTS = 13
        FLAG = 4
        row_mean = sb("row_mean", [P, 2])
        biases = sb("biases", [P, 2, 2, D])
        PARTS = 3
        KINDS = 4 * PARTS
        part_mask = sb("part_mask", [KINDS, 4, PARTS])
        bias_parts = sb("bias_parts", [KINDS, PARTS, 2, D], BF16)
        bias_rest = sb("bias_rest", [KINDS, 2, D])
        bias_rows = sb("bias_rows", [KINDS, 2, 2, D], BF16)
        part_ones = sb("part_ones", [PARTS, P], BF16)
        b2_block = sb("b2_block", [KINDS, 2, 4, D], BF16)
        tile_mask = sb("tile_mask", [KINDS, 4])
        kind_mask = sb("kind_mask", [KINDS, PARTS])
        biases_made = sem("biases_made")
        lines_counted = sem("lines_counted")
        early_done = sem("early_done")
        tile_ones = sb("tile_ones", [W, 4, KINDS], BF16)
        ident_b = sb("ident_b", [P, P], BF16)
        edge_counts = sb("edge_counts", [KINDS, GROUPS * P], BF16)
        MASKS = 11
        NODE_V = [5, 7, 8]
        EDGE_V, EDGE_T = 13, 6


        ones_col = sb("ones_col", [P, 1])
        node_iota = sb("node_iota", [P, 4, P])
        group_neg = sb("group_neg", [P, GROUPS])
        w2c = [sb(f"w2c_{l}", [P, D]) for l in range(2)]
        start_row = sb("start_row", [1, STARTS], I32)
        w_idx = sb("w_idx", [P, RING, 2], I32)
        w_xj = sb("w_xj", [P, RING, 2, D])
        w_x = sb("w_x", [P, RING, 4, D])
        w_win = sb("w_win", [P, RING, 4, D + 1])
        w_xf = sb("w_xf", [P, RING, 4, D])
        w_hj = sb("w_hj", [P, 2, 2, D])
        w_h = sb("w_h", [P, RING, 4, D])
        w_hjT = sb("w_hjT", [P, 2, P])
        w_b = sb("w_b", [P, 2, 2, D + 1])
        w_rel = sb("w_rel", [P, 4])
        w_oh = sb("w_oh", [P, RING, 4, P])
        w_ohT = sb("w_ohT", [P, 2, 4, W])
        w_xiT = sb("w_xiT", [P, 4 * W])
        w_z = sb("w_z", [P, 2, 4, D])
        w_hid = sb("w_hid", [P, 2, 4, D])
        w_agT = sb("w_agT", [P, 4 * P])
        w_sq = sb("w_sq", [P, 4, D])
        w_ssq = sb("w_ssq", [P, 2, 4])
        w_scaled = sb("w_scaled", [P, 2, 4, D])
        w_fin = sb("w_fin", [P, 2, 4, D])
        w_pos = sb("w_pos", [P, 2, 4, D])
        w_out = sb("w_out", [P, RING, 4, D])
        w_stats = sb("w_stats", [P, 6, 6])
        w_mean = sb("w_mean", [P, 6, 2])
        w_root = sb("w_root", [P, 10])
        w_inv = sb("w_inv", [P, 10])
        w_shift = sb("w_shift", [P, 6])
        p_ohT = psum[0][:, :, :].rearrange("p a b -> p (a b)").bitcast(BF16).rearrange("p (a b) -> p a b", a=4)
        p_y, p_h = (psum[4], psum[7]), psum[2]
        oh_b = w_oh[:, :, :, :].rearrange("p s j n -> p (s j n)").bitcast(BF16).rearrange("p (s j n h) -> p s j n h", s=RING, j=4, h=2)
        p_xiT = psum[1][:, :, :].rearrange("p a b -> p (a b)")[:, 0:4 * W]
        p_agT = psum[3][:, :, :].rearrange("p a b -> p (a b)")
        p_hjT, p_b, p_counts = psum[5][:, 0:2, :], psum[6][:, 0:2, :], psum[5][0:KINDS, 2, :]

        def per_layer(name):
            return [sem(f"{name}{l}") for l in range(2)]

        xj_in = [[sem(f"xj_in{l}_{k}") for k in range(RING)] for l in range(2)]
        x_in = [[sem(f"x_in{l}_{k}") for k in range(RING)] for l in range(2)]
        win_in = [[sem(f"win_in{l}_{k}") for k in range(RING)] for l in range(2)]
        xf_in = [sem(f"xf_in{k}") for k in range(RING)]
        b_out = [[sem(f"b_out{l}_{k}") for k in range(2)] for l in range(2)]
        stored = [[sem(f"stored{l}_{k}") for k in range(RING)] for l in range(2)]
        index_made = per_layer("index_made")
        stats_made, means_made = per_layer("stats_made"), per_layer("means_made")
        rooted, inv_made, shift_made = per_layer("rooted"), per_layer("inv_made"), per_layer("shift_made")
        hj_made, h_made = per_layer("hj_made"), per_layer("h_made")
        rel_made, oh_made = per_layer("rel_made"), per_layer("oh_made")
        oh_turned, ohT_copied = per_layer("oh_turned"), per_layer("ohT_copied")
        x_selected, xiT_copied = per_layer("x_selected"), per_layer("xiT_copied")
        h_summed, hid_made = per_layer("h_summed"), per_layer("hid_made")
        slope_made, windows_added = sem("slope_made"), per_layer("windows_added")
        aggregated, agT_copied, y_summed = per_layer("aggregated"), per_layer("agT_copied"), per_layer("y_summed")
        squared, scaled = per_layer("squared"), per_layer("scaled")
        biased, sloped, leaked = per_layer("biased"), sem("sloped"), per_layer("leaked")
        hj_turned, hjT_copied = per_layer("hj_turned"), per_layer("hjT_copied")
        b_summed, b_made = per_layer("b_summed"), per_layer("b_made")
        edges_counted, counts_copied = sem("edges_counted"), sem("counts_copied")

        def in_slot(slot):
            return (GROUPS - slot + RING - 1) // RING

        def root_active(l, s):
            return not s.static or (-1 if l == 0 else LAG + 3) <= s.n <= GROUPS + LAG + 2

        def root_count(l, s):
            return s.n + 1 - (-1 if l == 0 else LAG + 3)

        def rows_normalised(l, s):
            pair, nodes = l == 0 and (s + 1).active, l == 0 and (s - LAG + 2).active
            return (0 if pair else 2), (6 if nodes else 2)

        def wait_apart(eng, semaphore, value):
            eng.wait_ge(semaphore, value)
            eng.sem_inc(waited, 1)

        def sp_general(sp):
            def node_step(k, base, n):
                table = x if k == 0 else sums_dram
                sp.dma_start(g_rows[:, 0, :], table[bass.ds(base, P), :]).then_inc(node_in[k], 16)
                if k == 2:
                    sp.dma_start(g_x[:, :], x[bass.ds(base, P), :]).then_inc(node_in[k], 16)
                wait_apart(sp, node_vector[k], NODE_V[k] * n + NODE_V[k])
                target = (h_dram[0], h_dram[1], out)[k]
                sp.dma_start(target[bass.ds(base, P), :], g_node[:, 4, :]).then_inc(node_out[k], 16)
                wait_apart(sp, node_out[k], 16 * n + 16)

            sp.wait_ge(setup_done, 3)
            sp.wait_ge(early_done, 4)
            for half in range(2):
                sp.wait_ge(b_out[0][half], 16 * len(range(half, EARLY - 1, 2)))
            for k in range(3):
                if k:
                    sp.dma_start(sums_dram.rearrange("(t p) d -> p t d", p=P),
                                 g_zero[:, :].unsqueeze(1).to_broadcast([P, SUM_TILES, D])).then_inc(sums_zeroed, 16)
                    sp.wait_ge(edge_out[k - 1], 16 * EDGE_TILES)
                with sp.Fori(0, NODE_TILES - 1) as n:
                    node_step(k, n * P, n)
                node_step(k, LAST, NODE_TILES - 1)

        def pool_general(pool):
            pool.wait_ge(early_done, 4)
            for e in range(EARLY + 3):
                pool.wait_ge(xj_in[0][e % RING], 32 * (e // RING + 1))
            for l in range(2):
                pool.wait_ge(node_out[l], 16 * NODE_TILES)
                pool.wait_ge(sums_zeroed, 16 * (l + 1))
                with pool.Fori(0, EDGE_TILES) as t:
                    wait_apart(pool, edge_vector[l], EDGE_V * t + 7)
                    for c, table in enumerate((h_dram[l][0:N, :], h_dram[l][0:N, :], sums_dram)):
                        pool.indirect_dma_start(g_rows[:, c, :], None, table,
                                                bass.IndirectOffsetOnAxis(g_idx[:, c:c + 1], 0)).then_inc(edge_in[l], 16)
                    wait_apart(pool, edge_vector[l], EDGE_V * t + EDGE_V)
                    pool.indirect_dma_start(sums_dram, bass.IndirectOffsetOnAxis(g_idx[:, 2:3], 0),
                                            g_msg[:, 1, :], None).then_inc(edge_out[l], 16)
                    wait_apart(pool, edge_out[l], 16 * t + 16)

        def scalar_general(act):
            act.wait_ge(early_done, 4)
            for k in range(3):
                with act.Fori(0, NODE_TILES) as n:
                    act.wait_ge(node_vector[k], NODE_V[k] * n + 2)
                    nc.scalar.activation(g_root[:, 0:1], g_mean[:, 1:2], ACT.Sqrt,
                                         bias=eps_col[:, 0:1]).then_inc(node_root[k], 1)

        def vector_general(dve):
            dve.wait_ge(early_done, 4)
            def node_steps(k, n, steps):
                def step(ins):
                    steps[0] += 1
                    ins.then_inc(node_vector[k], 1)
                    wait_apart(dve, node_vector[k], NODE_V[k] * n + steps[0])

                dve.wait_ge(node_in[k], (16 if k < 2 else 32) * n + (16 if k < 2 else 32))
                step(nc.vector.bn_stats(g_stats[:, :], g_rows[:, 0, :]))
                step(nc.vector.bn_aggr(g_mean[:, :], g_stats[:, :]))
                dve.wait_ge(node_root[k], n + 1)
                step(nc.vector.reciprocal(g_root[:, 1:2], g_root[:, 0:1]))
                if k == 0:
                    step(nc.vector.tensor_scalar(g_node[:, 0, :], g_rows[:, 0, :], g_mean[:, 0:1], 0.0,
                                                 ALU.subtract, ALU.max))
                    step(nc.vector.tensor_scalar(g_node[:, 4, :], g_node[:, 0, :], g_root[:, 1:2], None, ALU.mult))
                    return
                step(nc.vector.tensor_scalar(g_node[:, 0, :], g_rows[:, 0, :], g_mean[:, 0:1], g_root[:, 1:2],
                                             ALU.subtract, ALU.mult))
                step(nc.vector.tensor_tensor(g_node[:, 1, :], g_node[:, 0, :], vecs[:, k - 1, 2, :], ALU.mult))
                step(nc.vector.tensor_tensor(g_node[:, 2, :], g_node[:, 1, :], vecs[:, k - 1, 3, :], ALU.add))
                last = g_node[:, 4, :] if k == 1 else g_node[:, 3, :]
                step(nc.vector.scalar_tensor_tensor(last, g_node[:, 2, :], SLOPE, g_node[:, 2, :], ALU.mult, ALU.max))
                if k == 2:
                    step(nc.vector.tensor_tensor(g_node[:, 4, :], g_node[:, 3, :], g_x[:, :], ALU.add))

            def edge_steps(l, t):
                count = [0]

                def step(ins):
                    count[0] += 1
                    ins.then_inc(edge_vector[l], 1)
                    wait_apart(dve, edge_vector[l], EDGE_V * t + count[0])

                dst_col = dst_cols[:, bass.ds(t, 1)]
                step(nc.vector.tensor_copy(g_key[:, :], dst_col.to_broadcast([P, P])))
                step(nc.vector.tensor_copy(g_idx[:, 1:2], src_cols[:, bass.ds(t, 1)]))
                step(nc.vector.tensor_scalar(g_idx[:, 0:1], dst_col, float(N - 1), None, ALU.min))
                dve.wait_ge(edge_tensor[l], EDGE_T * t + 1)
                step(nc.vector.tensor_scalar(g_same[:, 0, :], psum[0][:, 0, :], dst_col, None, ALU.is_equal))
                step(nc.vector.tensor_tensor_reduce(g_same[:, 1, :], g_same[:, 0, :], earlier[:, :], 1.0, 0.0,
                                                    ALU.mult, ALU.max, g_col[:, 0:1]))
                step(nc.vector.tensor_scalar(g_col[:, 1:2], lane_dump[:, :], dst_col, g_col[:, 0:1],
                                             ALU.subtract, ALU.mult))
                step(nc.vector.tensor_scalar(g_idx[:, 2:3], dst_col, g_col[:, 1:2], None, ALU.add))
                dve.wait_ge(edge_tensor[l], EDGE_T * t + 2)
                step(nc.vector.tensor_copy(g_hT[:, :, :], psum[1][:, 0:2, :]))
                dve.wait_ge(edge_tensor[l], EDGE_T * t + 3)
                step(nc.vector.tensor_tensor(g_hid[:, 0, :], psum[2][:, 0, :], vecs[:, l, 0, :], ALU.add))
                step(nc.vector.scalar_tensor_tensor(g_hid[:, 1, :], g_hid[:, 0, :], SLOPE, g_hid[:, 0, :],
                                                    ALU.mult, ALU.max))
                dve.wait_ge(edge_tensor[l], EDGE_T * t + 4)
                step(nc.vector.tensor_copy(g_hidT[:, :], psum[3][:, 0, :]))
                dve.wait_ge(edge_tensor[l], EDGE_T * t + 5)
                step(nc.vector.tensor_tensor(g_msg[:, 0, :], psum[4][:, 0, :], vecs[:, l, 1, :], ALU.add))
                dve.wait_ge(edge_tensor[l], EDGE_T * t + 6)
                step(nc.vector.tensor_tensor(g_msg[:, 1, :], psum[5][:, 0, :], g_rows[:, 2, :], ALU.add))
                assert count[0] == EDGE_V

            for k in range(3):
                if k:
                    with dve.Fori(0, EDGE_TILES) as t:
                        edge_steps(k - 1, t)
                        dve.wait_ge(edge_out[k - 1], 16 * t + 16)
                with dve.Fori(0, NODE_TILES) as n:
                    node_steps(k, n, [0])
                    dve.wait_ge(node_out[k], 16 * n + 16)

        def tensor_general(pe):
            pe.wait_ge(early_done, 4)
            for l in range(2):
                with pe.Fori(0, EDGE_TILES) as t:
                    def after(dve_steps):
                        pe.wait_ge(edge_vector[l], EDGE_V * t + dve_steps)
                    after(1)
                    nc.tensor.transpose(psum[0][:, 0, :], g_key[:, :], ident[:, :]).then_inc(edge_tensor[l], 1)
                    pe.wait_ge(edge_in[l], 48 * t + 48)
                    for c in range(2):
                        last = nc.tensor.transpose(psum[1][:, c, :], g_rows[:, c, :], ident[:, :])
                    last.then_inc(edge_tensor[l], 1)
                    after(8)
                    nc.tensor.matmul(psum[2][:, 0, :], g_hT[:, 0, :], w1d[l][:, :], start=True, stop=False)
                    nc.tensor.matmul(psum[2][:, 0, :], g_hT[:, 1, :], w1[l][:, 1, :], start=False,
                                     stop=True).then_inc(edge_tensor[l], 1)
                    after(10)
                    nc.tensor.transpose(psum[3][:, 0, :], g_hid[:, 1, :], ident[:, :]).then_inc(edge_tensor[l], 1)
                    after(11)
                    nc.tensor.matmul(psum[4][:, 0, :], g_hidT[:, :], w2[l][:, :], start=True,
                                     stop=True).then_inc(edge_tensor[l], 1)
                    after(12)
                    nc.tensor.matmul(psum[5][:, 0, :], g_same[:, 0, :], g_msg[:, 0, :], start=True,
                                     stop=True).then_inc(edge_tensor[l], 1)


        def need(eng, semaphore, count):
            if not isinstance(count, int) or count > 0:
                eng.wait_ge(semaphore, count)

        def need_apart(eng, semaphore, count):
            if not isinstance(count, int):
                wait_apart(eng, semaphore, count)
            elif count > 0:
                eng.wait_ge(semaphore, count)

        def run_steps(eng, step, first):
            for s in range(first, LOOP_FROM):
                step(Group(0, s))
            with eng.Fori(0, LOOPS) as i:
                for u in range(RING):
                    step(Group(i, LOOP_FROM + u))
            for s in range(LOOP_FROM + RING * LOOPS, LAST_STEP + 1):
                step(Group(0, s))

        def load_nodes(eng, table, to, g, signal):
            if table is x and g.last:
                whole = (N - g.n * 4 * P) // P
                for j in range(whole):
                    eng.dma_start(to[:, g.slot, j, :], x[g.n * 4 * P + j * P:g.n * 4 * P + (j + 1) * P, :]).then_inc(signal[g.slot], 16)
                eng.dma_start(to[0:N % P, g.slot, whole, :], x[N - N % P:N, :]).then_inc(signal[g.slot], 16)
            else:
                eng.dma_start(to[:, g.slot, :, :],
                              table[bass.ds(g.n * (4 * P), 4 * P), :].rearrange("(j p) d -> p j d", p=P)).then_inc(signal[g.slot], 16)

        def store_nodes(eng, l, o):
            if l == 1 and o.last:
                whole = (N - o.n * 4 * P) // P
                eng.dma_start(out[o.n * 4 * P:o.n * 4 * P + whole * P, :].rearrange("(j p) d -> p j d", p=P),
                              w_out[:, o.slot, 0:whole, :]).then_inc(stored[l][o.slot], 16)
                eng.dma_start(out[N - N % P:N, :], w_out[0:N % P, o.slot, whole, :]).then_inc(stored[l][o.slot], 16)
            else:
                eng.dma_start((h_dram[1], out)[l][bass.ds(o.n * (4 * P), 4 * P), :].rearrange("(j p) d -> p j d", p=P),
                              w_out[:, o.slot, :, :]).then_inc(stored[l][o.slot], 16)

        def store_pair(eng, l, e):
            need_apart(eng, b_made[l], e.n + 1)
            eng.dma_start(b_dram[bass.ds(e.n * ROW, ROW), :].rearrange("(k p) d -> p k d", p=P),
                          w_b[:, e.half, :, :]).then_inc(b_out[l][e.half], 16)

        def sp_steps(sp, l):
            nodes = x if l == 0 else h_dram[1]
            starts = [sp.alloc_register(f"start{l}_{j}") for j in range(4)]

            def step(s):
                a = s - LAG
                g = a + 3
                if g.active:
                    need_apart(sp, h_made[l] if l == 0 else x_selected[l], g.n - 3)
                    load_nodes(sp, nodes, w_x, g, x_in[l])
                w = a + 3
                if w.active:
                    sp.load(starts, start_row[0:1, bass.ds(w.n * 4, 4)])
                    need_apart(sp, windows_added[l], w.n - 3)
                    p = w + 2 if not w.static or w.n + 2 < PAIRS else Group(0, PAIRS - 1)
                    need_apart(sp, b_out[l][0], (p.n2 + 1) * 16)
                    need_apart(sp, b_out[l][1], ((p + 1).n2) * 16)
                    for j in range(4):
                        at = sp.snap(starts[j], min_val=0, max_val=E)
                        sp.dma_start(w_win[0:W, w.slot, j, :], b_dram[bass.ds(at, W), :]).then_inc(win_in[l][w.slot], 16)
                e, o = s - 1, a - 6
                if l == 0 and e.active:
                    store_pair(sp, l, e)
                if o.active:
                    need_apart(sp, leaked[l], o.n + 1)
                    store_nodes(sp, l, o)

            return step

        def all_stored(sp, l):
            for slot in range(RING):
                sp.wait_ge(stored[l][slot], 16 * in_slot(slot) + (16 if l == 1 and slot == (GROUPS - 1) % RING else 0))
            for half in range(2):
                sp.wait_ge(b_out[l][half], 16 * (PAIRS // 2))

        def pool_steps(pool, l):
            table = x if l == 0 else h_dram[1][0:N, :]
            b_all = vecs[:, l, 3, :].unsqueeze(1).to_broadcast([P, 4, D])

            def step(s):
                e, e1, a = s + 3, s + 1, s - LAG
                f = a - 3
                if l == 0 and e1.active:
                    need_apart(pool, shift_made[l], root_count(l, s))
                    need_apart(pool, hj_turned[l], e1.n - 1)
                    for k in range(2):
                        last = pool.tensor_scalar(w_hj[:, e1.half, k, :], w_xj[:, e1.slot, k, :], w_inv[:, k:k + 1],
                                                  w_shift[:, k:k + 1], ALU.mult, ALU.add)
                    last.then_inc(hj_made[l], 1)
                if f.active:
                    need_apart(pool, leaked[l] if l == 0 else sloped, f.n - 1)
                    need_apart(pool, scaled[l], f.n + 1)
                    pool.tensor_tensor(w_fin[:, f.half, :, :], w_scaled[:, f.half, :, :], b_all, ALU.add).then_inc(biased[l], 1)
                if e.active:
                    if not e.static or e.n >= RING:
                        need_apart(pool, xj_in[l][e.slot], e.q * 32)
                    pool.tensor_copy(w_idx[:, e.slot, :], src_cols[:, bass.ds(e.n * 2, 2)]).then_inc(index_made[l], 1)
                    need_apart(pool, hj_made[l] if l == 0 else hj_turned[l], e.n - 3)
                    need_apart(pool, index_made[l], e.n + 1)
                    for k in range(2):
                        pool.indirect_dma_start(w_xj[:, e.slot, k, :], None, table,
                                                bass.IndirectOffsetOnAxis(w_idx[:, e.slot, k:k + 1], 0)).then_inc(xj_in[l][e.slot], 16)

            return step

        def scalar_steps(act, l):
            selected = ACT.Relu if l == 0 else ACT.Copy

            def normalise(n, first):
                for j in range(first, first + 2):
                    last = nc.scalar.activation(w_h[:, n.slot, j, :], w_x[:, n.slot, j, :], ACT.Identity,
                                                bias=w_shift[:, 2 + j:3 + j], scale=w_inv[:, 2 + j:3 + j])
                return last

            def take_roots(s):
                if root_active(l, s):
                    lo, hi = rows_normalised(l, s)
                    f = s - LAG - 3
                    need(act, inv_made[l], root_count(l, s) - 1)
                    if lo < hi:
                        act.wait_ge(means_made[l], root_count(l, s))
                        last = nc.scalar.activation(w_root[:, lo:hi], w_mean[:, lo:hi, 1], ACT.Sqrt, bias=eps_col[:, 0:1])
                    if f.active:
                        act.wait_ge(squared[l], f.n + 1)
                        last = nc.scalar.activation(w_root[:, 6:10], w_ssq[:, f.half, :], ACT.Sqrt, bias=eps_col[:, 0:1],
                                                    scale=1.0 / D)
                    last.then_inc(rooted[l], 1)

            def step(s):
                e, a = s, s - LAG
                t, n, g, q, eb = a + 1, a + 2, a - 1, a - 2, s - 1
                if l == 0 and t.active:
                    normalise(t, 2).then_inc(h_made[l], 1)
                if a.active:
                    act.wait_ge(x_selected[l], a.n + 1)
                    need(act, h_summed[l], a.n)
                    nc.scalar.activation(w_xiT[:, :], p_xiT[:, :], selected).then_inc(xiT_copied[l], 1)
                if eb.active:
                    if not eb.static or eb.n >= 2:
                        act.wait_ge(b_out[l][eb.half], eb.n2 * 16)
                    nc.scalar.activation(w_b[:, eb.half, :, D], dst_cols[:, bass.ds(eb.n * 2, 2)], ACT.Copy)
                    act.wait_ge(b_summed[l], eb.n + 1)
                    nc.scalar.activation(w_b[:, eb.half, :, 0:D], p_b, ACT.Copy).then_inc(b_made[l], 1)
                if l == 0:
                    take_roots(s)
                if g.active:
                    act.wait_ge(aggregated[l], g.n + 1)
                    need(act, y_summed[l], g.n)
                    nc.scalar.activation(w_agT[:, :], p_agT[:, :], ACT.Copy).then_inc(agT_copied[l], 1)
                if l == 0 and t.active:
                    act.wait_ge(edges_counted, t.n + 1)
                    if e.active:
                        act.wait_ge(hj_turned[l], e.n + 1)
                    nc.scalar.activation(edge_counts[:, bass.ds(t.n * P, P)], p_counts, ACT.Copy).then_inc(counts_copied, 1)
                if e.active:
                    act.wait_ge(hj_turned[l], e.n + 1)
                    need(act, b_summed[l], e.n)
                    nc.scalar.activation(w_hjT[:, :, :], p_hjT, selected).then_inc(hjT_copied[l], 1)
                if l == 0 and a.active:
                    act.wait_ge(h_summed[l], a.n + 1)
                    need(act, hid_made[l], a.n - 1)
                    nc.scalar.activation(w_z[0:W, a.half, 0:PE_ADDS, :], p_h[0:W, 0:PE_ADDS, :], ACT.Copy,
                                         scale=SLOPE).then_inc(slope_made, 1)
                if l == 0 and n.active:
                    act.wait_ge(shift_made[l], root_count(l, s))
                    need(act, x_selected[l], n.n - 3)
                    normalise(n, 0)
                if t.active:
                    act.wait_ge(oh_turned[l], t.n + 1)
                    need(act, x_selected[l], t.n - 1)
                    nc.scalar.activation(w_ohT[:, t.half, :, :], p_ohT[:, :, 0:W], ACT.Copy).then_inc(ohT_copied[l], 1)
                if q.active:
                    act.wait_ge(y_summed[l], q.n + 1)
                    for j in range(4):
                        last = nc.scalar.activation(w_sq[:, j, :], p_y[q.half][:, j, :], ACT.Square,
                                                    accum_out=w_ssq[:, q.half, j:j + 1])
                    last.then_inc(squared[l], 1)
                if l == 1:
                    v = a - 3
                    if eb.active:
                        store_pair(act, l, eb)
                    if v.active:
                        need_apart(act, leaked[l], v.n - 3)
                        load_nodes(act, x, w_xf, v, xf_in)
                    take_roots(s + 1)

            return step

        def vector_steps(dve, l):
            g_all = vecs[:, l, 2, :]

            def invert(s):
                if root_active(l, s):
                    dve.wait_ge(rooted[l], root_count(l, s))
                    if l == 0:
                        need(dve, hj_made[l], (s + 1).before)
                        need(dve, h_made[l], (s - LAG + 2).before)
                    cols = slice(0, 10) if l == 0 else slice(6, 10)
                    nc.vector.reciprocal(w_inv[:, cols], w_root[:, cols]).then_inc(inv_made[l], 1)

            def leaky(o):
                if o.active:
                    dve.wait_ge(biased[l], o.n + 1)
                    if l == 0:
                        if not o.static or o.n >= RING:
                            dve.wait_ge(stored[l][o.slot], o.q * 16)
                        to, signal = w_out[:, o.slot, :, :], leaked[l]
                    else:
                        need(dve, leaked[l], o.n - 1)
                        to, signal = w_pos[:, o.half, :, :], sloped
                    nc.vector.scalar_tensor_tensor(to, w_fin[:, o.half, :, :], SLOPE, w_fin[:, o.half, :, :], ALU.mult,
                                                   ALU.max).then_inc(signal, 1)

            def step(s):
                e, a = s, s - LAG
                e1, a2, f, o, d = s + 1, a + 2, a - 3, a - 4, a - 5
                norm_pair, norm_nodes = l == 0 and e1.active, l == 0 and a2.active
                if norm_pair:
                    dve.wait_ge(xj_in[l][e1.slot], (e1.q + 1) * 32)
                    for k in range(2):
                        last = nc.vector.bn_stats(w_stats[:, k, :], w_xj[:, e1.slot, k, :])
                if norm_nodes:
                    dve.wait_ge(x_in[l][a2.slot], (a2.q + 1) * 16 + (LAST_LOADS * 16 - 16 if a2.last else 0))
                    for j in range(4):
                        last = nc.vector.bn_stats(w_stats[:, 2 + j, :], w_x[:, a2.slot, j, :])
                if norm_pair or norm_nodes:
                    last.then_inc(stats_made[l], 1)
                if a2.active:
                    dve.wait_ge(win_in[l][a2.slot], (a2.q + 1) * 64)
                    need(dve, oh_made[l], a2.n)
                    nc.vector.tensor_scalar(w_rel[0:W, :], w_win[0:W, a2.slot, :, D], group_neg[0:W, bass.ds(a2.n, 1)], None,
                                            ALU.add).then_inc(rel_made[l], 1)
                if l == 1 and d.active:
                    dve.wait_ge(sloped, d.n + 1)
                    if not d.static or d.n >= RING:
                        dve.wait_ge(stored[l][d.slot], d.q * 16)
                    dve.wait_ge(xf_in[d.slot], (d.q + 1) * 16 + (LAST_LOADS * 16 - 16 if d.last else 0))
                    nc.vector.tensor_tensor(w_out[:, d.slot, :, :], w_pos[:, d.half, :, :], w_xf[:, d.slot, :, :],
                                            ALU.add).then_inc(leaked[l], 1)
                if norm_pair or norm_nodes:
                    need_apart(dve, stats_made[l], root_count(l, s))
                    lo, hi = rows_normalised(l, s)
                    for k in range(lo, hi):
                        last = nc.vector.bn_aggr(w_mean[:, k, :], w_stats[:, k, :])
                    last.then_inc(means_made[l], 1)
                if a2.active:
                    need(dve, y_summed[l], a2.n - 3)
                    dve.wait_ge(rel_made[l], a2.n + 1)
                    nc.vector.tensor_tensor(w_oh[0:W, a2.slot, :, :], node_iota[0:W, :, :],
                                            w_rel[0:W, :].unsqueeze(2).to_broadcast([W, 4, P]), ALU.is_equal).then_inc(oh_made[l], 1)
                if l == 0:
                    leaky(o)
                invert(s)
                if root_active(l, s):
                    dve.wait_ge(inv_made[l], root_count(l, s))
                if norm_pair or norm_nodes:
                    nc.vector.scalar_tensor_tensor(w_shift[:, :], w_mean[:, :, 0], -1.0, w_inv[:, 0:6], ALU.mult,
                                                   ALU.mult).then_inc(shift_made[l], 1)
                if f.active:
                    need(dve, biased[l], f.n - 1)
                    for j in range(4):
                        last = nc.vector.scalar_tensor_tensor(w_scaled[:, f.half, j, :], p_y[f.half][:, j, :], w_inv[:, 6 + j:7 + j],
                                                              g_all, ALU.mult, ALU.mult)
                    last.then_inc(scaled[l], 1)
                added = PE_ADDS if l == 0 else 0
                if a.active:
                    dve.wait_ge(h_summed[l], a.n + 1)
                    if added:
                        dve.wait_ge(slope_made, a.n + 1)
                    need(dve, hid_made[l], a.n - 1)
                    nc.vector.tensor_tensor(w_z[0:W, a.half, added:4, :], p_h[0:W, added:4, :], w_win[0:W, a.slot, added:4, 0:D],
                                            ALU.add).then_inc(windows_added[l], 1)
                if l == 1:
                    leaky(o)
                if a.active:
                    need(dve, aggregated[l], a.n - 1)
                    if added:
                        nc.vector.tensor_tensor(w_hid[0:W, a.half, 0:added, :], p_h[0:W, 0:added, :], w_z[0:W, a.half, 0:added, :],
                                                ALU.max)
                    dve.wait_ge(windows_added[l], a.n + 1)
                    nc.vector.scalar_tensor_tensor(w_hid[0:W, a.half, added:4, :], w_z[0:W, a.half, added:4, :], SLOPE,
                                                   w_z[0:W, a.half, added:4, :], ALU.mult, ALU.max).then_inc(hid_made[l], 1)

            return step

        def tensor_steps(pe, l):
            w1b = w1[l][:, 1, :]

            def step(s):
                e, a = s, s - LAG
                t, g = a + 1, a - 1
                if a.active:
                    pe.wait_ge(ohT_copied[l], a.n + 1)
                    need(pe, xiT_copied[l], a.n)
                    if l == 0:
                        pe.wait_ge(h_made[l], a.n + 1)
                    else:
                        pe.wait_ge(x_in[l][a.slot], (a.q + 1) * 16)
                    for j in range(4):
                        rows = w_h[:, a.slot, j, :] if l == 0 else w_x[:, a.slot, j, :]
                        last = nc.tensor.matmul(p_xiT[:, j * W:(j + 1) * W], rows, w_ohT[:, a.half, j, :], start=True, stop=True)
                    last.then_inc(x_selected[l], 1)
                if g.active:
                    pe.wait_ge(hid_made[l], g.n + 1)
                    need(pe, agT_copied[l], g.n)
                    for j in range(4):
                        last = nc.tensor.matmul(p_agT[:, j * P:(j + 1) * P], w_hid[0:W, g.half, j, :], w_oh[0:W, g.slot, j, :],
                                                start=True, stop=True)
                    last.then_inc(aggregated[l], 1)
                if l == 0 and t.active:
                    need(pe, counts_copied, t.n)
                    need(pe, hjT_copied[l], e.before)
                    pe.wait_ge(oh_made[l], t.n + 1)
                    for j in range(4):
                        last = nc.tensor.matmul(p_counts, tile_ones[:, j, :], oh_b[0:W, t.slot, j, :, 1], start=(j == 0), stop=(j == 3))
                    last.then_inc(edges_counted, 1)
                if e.active:
                    if l == 0:
                        need(pe, counts_copied, t.n)
                        pe.wait_ge(hj_made[l], e.n + 1)
                    else:
                        pe.wait_ge(xj_in[l][e.slot], (e.q + 1) * 32)
                    need(pe, hjT_copied[l], e.n)
                    for k in range(2):
                        rows = w_hj[:, e.half, k, :] if l == 0 else w_xj[:, e.slot, k, :]
                        last = nc.tensor.transpose(p_hjT[:, k, :], rows, ident[:, :])
                    last.then_inc(hj_turned[l], 1)
                if a.active:
                    pe.wait_ge(xiT_copied[l], a.n + 1)
                    need(pe, hid_made[l], a.n)
                    for j in range(4):
                        with_window = l == 0 and j < PE_ADDS
                        last = nc.tensor.matmul(p_h[0:W, j, :], w_xiT[:, j * W:(j + 1) * W], w1d[l][:, :], start=True,
                                                stop=not with_window)
                        if with_window:
                            last = nc.tensor.matmul(p_h[0:W, j, :], ident[0:W, 0:W], w_win[0:W, a.slot, j, 0:D], start=False, stop=True)
                    last.then_inc(h_summed[l], 1)
                if e.active:
                    need(pe, b_made[l], e.n)
                    if e.static:
                        pe.wait_ge(biases_made, l + 1)
                    nc.tensor.matmul(p_b, part_ones[:, :], bias_rows[0:PARTS, l, 0, :].unsqueeze(1).to_broadcast([PARTS, 2, D]),
                                     start=True, stop=False)
                    pe.wait_ge(hjT_copied[l], e.n + 1)
                    for k in range(2):
                        last = nc.tensor.matmul(p_b[:, k, :], w_hjT[:, k, :], w1b, start=False, stop=(k == 1))
                    last.then_inc(b_summed[l], 1)
                if t.active:
                    pe.wait_ge(oh_made[l], t.n + 1)
                    need(pe, ohT_copied[l], t.n)
                    for j in range(4):
                        last = nc.tensor.transpose(p_ohT[:, j, 0:W], oh_b[0:W, t.slot, j, :, 1], ident_b[0:W, 0:W])
                    last.then_inc(oh_turned[l], 1)
                if g.active:
                    if l == 0:
                        pe.wait_ge(counts_copied, g.n + 1)
                    need(pe, scaled[l], g.n - 1)
                    nc.tensor.matmul(p_y[g.half][:, :, :], edge_counts[:, bass.ds(g.n * P, P)], b2_block[:, l, :, :], start=True, stop=False)
                    pe.wait_ge(agT_copied[l], g.n + 1)
                    for j in range(4):
                        last = nc.tensor.matmul(p_y[g.half][:, j, :], w_agT[:, j * P:(j + 1) * P], w2c[l][:, :], start=False,
                                                stop=(j == 3))
                    last.then_inc(y_summed[l], 1)

            return step

        block = ctx.enter_context(nc.Block())

        @block.sync
        def _(sp):
            sp.wait_ge(masks_made, MASKS)
            full, rest = E // ROW, E % ROW
            for c, a in enumerate((src, dst)):
                sp.dma_start(edge_rows[0:full, c, :],
                             a[0:full * ROW].rearrange("(p c) -> p c", c=ROW)).then_inc(edges_loaded, 16)
                sp.dma_start(edge_rows[full:PAIRS, c, 0:rest],
                             a[full * ROW:E].rearrange("(p c) -> p c", p=1)).then_inc(edges_loaded, 16)
            sp.dma_start(next_in[0:full, :], dst[1:full * ROW + 1].rearrange("(p c) -> p c", c=ROW)).then_inc(edges_loaded, 16)
            sp.dma_start(next_in[full:PAIRS, 0:rest - 1],
                         dst[full * ROW + 1:E].rearrange("(p c) -> p c", p=1)).then_inc(edges_loaded, 16)
            for l in range(2):
                W1, b1, W2, b2, g, b = weights[l]
                sp.dma_start(w1[l][:, :, :], W1.rearrange("(a p) n -> p a n", a=2)).then_inc(weights_loaded, 16)
                sp.dma_start(w2[l][:, :], W2).then_inc(weights_loaded, 16)
                for c, v in enumerate((b1, b2, g, b)):
                    sp.dma_start(vec_row[0:1, l, c, :], v.rearrange("(a d) -> a d", a=1)).then_inc(weights_loaded, 16)
            sp.wait_ge(masks_made, MASKS)
            sp.wait_ge(blank_set, 2)
            sp.dma_start(b_dram[PAIRS * ROW:, :].rearrange("(k p) d -> p k d", p=P), b_blank[:, :, :]).then_inc(b_padded, 16)
            sp.wait_ge(table_made, 1)
            sp.dma_start(starts_dram.rearrange("(q r) -> q r", q=LINES), start_table[:, :]).then_inc(starts_out, 16)
            sp.wait_ge(starts_out, 16)
            sp.dma_start(start_row[:, :], starts_dram.rearrange("(a n) -> a n", a=1)).then_inc(starts_in, 16)
            sp.wait_ge(b_padded, 16)
            pair_step = sp_steps(sp, 0)
            for s in range(FIRST, EARLY):
                pair_step(Group(0, s))
            sp.sem_inc(early_done, 1)
            sp.wait_ge(flag_made, 1)
            ok = sp.value_load(flag[0:1, 0:1], min_val=0, max_val=1)
            with sp.If(ok == 1):
                run_steps(sp, pair_step, EARLY)
                all_stored(sp, 0)
                run_steps(sp, sp_steps(sp, 1), FIRST)
                all_stored(sp, 1)
            with sp.Else():
                sp_general(sp)

        @block.gpsimd
        def _(pool):
            pool.memset(edge_rows[:, 0, :], 0).then_inc(masks_made, 1)
            pool.iota(edge_rows[:, 1, :].rearrange("p (a c) -> p a c", a=2), pattern=[[0, 2], [1, P]],
                      base=NPAD, channel_multiplier=0).then_inc(masks_made, 1)
            pool.iota(lane_dump[:, :], pattern=[[0, 1]], base=NPAD, channel_multiplier=1,
                      allow_small_or_imprecise_dtypes=True).then_inc(blanks_made, 1)
            pool.memset(ident[:, :], 0.0).then_inc(blanks_made, 1)
            pool.memset(earlier[:, :], 1.0).then_inc(blanks_made, 1)
            pool.memset(part_mask[:, :, :], 0.0).then_inc(blanks_made, 1)
            pool.memset(lower_lines[:, :], 1.0).then_inc(blanks_made, 1)
            pool.wait_ge(blanks_made, 5)
            pool.affine_select(out=lower_lines[:, :], in_=lower_lines[:, :], compare_op=ALU.is_gt, fill=0.0, base=0,
                               pattern=[[1, LINES]], channel_multiplier=-1).then_inc(masks_made, 1)
            pool.affine_select(out=part_mask[:, :, :], in_=part_mask[:, :, :], compare_op=ALU.not_equal, fill=1.0, base=0,
                               pattern=[[-PARTS, 4], [-1, PARTS]], channel_multiplier=1).then_inc(masks_made, 1)
            pool.affine_select(out=ident[:, :], in_=ident[:, :], compare_op=ALU.not_equal, fill=1.0, base=0,
                               pattern=[[-1, P]], channel_multiplier=1).then_inc(masks_made, 1)
            pool.affine_select(out=earlier[:, :], in_=earlier[:, :], compare_op=ALU.is_gt, fill=0.0, base=0,
                               pattern=[[-1, P]], channel_multiplier=1).then_inc(masks_made, 1)
            pool.memset(next_in[:, :], int(PAD)).then_inc(masks_made, 1)
            pool.iota(node_iota[:, :, :], pattern=[[P, 4], [1, P]], base=0, channel_multiplier=0,
                      allow_small_or_imprecise_dtypes=True).then_inc(masks_made, 1)
            pool.iota(group_neg[:, :], pattern=[[-4 * P, GROUPS]], base=0, channel_multiplier=0,
                      allow_small_or_imprecise_dtypes=True).then_inc(masks_made, 1)
            pool.iota(number[:, :], pattern=[[1, LINES]], base=0, channel_multiplier=0,
                      allow_small_or_imprecise_dtypes=True).then_inc(masks_made, 1)
            pool.iota(even_rate[:, :], pattern=[[P * E // N, NODE_TILES]], base=0, channel_multiplier=0,
                      allow_small_or_imprecise_dtypes=True).then_inc(masks_made, 1)
            pool.memset(b_blank[:, :, 0:D], 0.0).then_inc(blank_set, 1)
            pool.memset(b_blank[:, :, D:D + 1], -1.0).then_inc(blank_set, 1)
            pair_step = pool_steps(pool, 0)
            pool.wait_ge(cols_made, 4)
            for s in range(FIRST, EARLY):
                pair_step(Group(0, s))
            pool.sem_inc(early_done, 1)
            pool.wait_ge(flag_made, 1)
            ok = pool.value_load(flag[0:1, 0:1], min_val=0, max_val=1)
            with pool.If(ok == 1):
                run_steps(pool, pair_step, EARLY)
                for slot in range(RING):
                    pool.wait_ge(stored[0][slot], 16 * in_slot(slot))
                run_steps(pool, pool_steps(pool, 1), FIRST)
            with pool.Else():
                pool_general(pool)

        @block.scalar
        def _(act):
            pair_step = scalar_steps(act, 0)
            act.wait_ge(cols_made, 4)
            for s in range(FIRST, EARLY):
                pair_step(Group(0, s))
            act.sem_inc(early_done, 1)
            act.wait_ge(flag_made, 1)
            ok = act.value_load(flag[0:1, 0:1], min_val=0, max_val=1)
            with act.If(ok == 1):
                run_steps(act, pair_step, EARLY)
                run_steps(act, scalar_steps(act, 1), FIRST)
            with act.Else():
                scalar_general(act)

        @block.vector
        def _(dve):
            nc.vector.memset(eps_col[:, :], EPS).then_inc(consts_set, 1)
            nc.vector.memset(g_zero[:, :], 0.0).then_inc(consts_set, 1)
            nc.vector.memset(ones_row[:, :], 1.0).then_inc(consts_set, 1)
            nc.vector.memset(ones_col[:, :], 1.0).then_inc(consts_set, 1)
            nc.vector.memset(part_ones[:, :], 1.0).then_inc(consts_set, 1)
            nc.vector.memset(below_col[:, :, COLS:COLS + 1], 1.0).then_inc(consts_set, 1)
            nc.vector.memset(w_root[:, :], 1.0).then_inc(consts_set, 1)
            nc.vector.memset(w_mean[:, :, :], 0.0).then_inc(consts_set, 1)
            nc.vector.memset(w_x[:, :, :, :], 0.0).then_inc(consts_set, 1)
            nc.vector.memset(tile_ones[:, :, :], 0.0).then_inc(counted, 1)
            dve.wait_ge(counted, 1)
            for j in range(4):
                nc.vector.memset(tile_ones[:, j, PARTS * j:PARTS * (j + 1)], 1.0).then_inc(consts_set, 1)

            hands = [0]

            def step(ins):
                hands[0] += 1
                ins.then_inc(hand, 1)
                dve.wait_ge(hand, hands[0])

            dve.wait_ge(edges_loaded, 96)
            nc.vector.tensor_copy(edge_rows_f[:, :, :], edge_rows[:, :, :]).then_inc(edges_cast, 1)
            step(nc.vector.tensor_copy(next_rows[:, :], next_in[:, :]))
            dve.wait_ge(edges_cast, 1)
            step(nc.vector.tensor_tensor(down[:, :], edge_rows_f[:, 1, :], next_rows[:, :], ALU.is_gt))
            nc.vector.tensor_reduce(downs[:, :], down[:, :], AX.X, ALU.add).then_inc(downs_made, 1)
            dve.wait_ge(turned, 1)
            for k in range(2):
                nc.vector.tensor_copy(src_cols[:, k:EDGE_TILES:2], psum[k][:, 0, 0:PAIRS]).then_inc(cols_made, 1)
                nc.vector.tensor_copy(dst_cols[:, k:EDGE_TILES:2], psum[k][:, 1, 0:PAIRS]).then_inc(cols_made, 1)
            dve.wait_ge(cols_made, 4)
            dve.wait_ge(masks_made, MASKS)

            nc.vector.tensor_copy(ident_b[:, :], ident[:, :]).then_inc(cols_made, 1)
            step(nc.vector.tensor_copy(dst_int[:, 0, :], dst_cols[:, :]))
            nc.vector.tensor_scalar(dst_int[:, 1, :], dst_int[:, 0, :], PB + CB, None, ALU.arith_shift_right).then_inc(parts_made, 1)
            nc.vector.tensor_scalar(dst_int[:, 2, :], dst_int[:, 0, :], PB, COLS - 1, ALU.arith_shift_right,
                                    ALU.bitwise_and).then_inc(parts_made, 1)
            dve.wait_ge(parts_made, 2)
            step(nc.vector.tensor_copy(dst_part[:, :, :], dst_int[:, 1:3, :]))
            def compare(half):
                ts = slice(half * PAIRS, (half + 1) * PAIRS)
                for to, part, width, op in ((in_line, 0, LINES, ALU.is_equal), (below_col, 1, COLS, ALU.is_lt)):
                    last = nc.vector.tensor_tensor(to[:, ts, 0:width], dst_part[:, part, ts].unsqueeze(2).to_broadcast([P, PAIRS, width]),
                                                   number[:, 0:width].unsqueeze(1).to_broadcast([P, PAIRS, width]), op)
                last.then_inc(counted, 1)

            def derive_weights(l):
                nc.vector.tensor_tensor(w1d[l][:, :], w1[l][:, 0, :], w1[l][:, 1, :], ALU.subtract).then_inc(cols_made, 1)
                for whole, less in ((w2[l][:, :], w2c[l][:, :]), (vecs[:, l, 1, :], biases[:, l, 1, :])):
                    step(nc.vector.tensor_reduce(row_mean[:, 0:1], whole, AX.X, ALU.add))
                    step(nc.vector.tensor_scalar(row_mean[:, 1:2], row_mean[:, 0:1], 1.0 / D, None, ALU.mult))
                    step(nc.vector.tensor_scalar(less, whole, row_mean[:, 1:2], None, ALU.subtract))
                step(nc.vector.tensor_copy(biases[:, l, 0, :], vecs[:, l, 0, :]))
                step(nc.vector.tensor_copy(bias_parts[:, 0, :, :], biases[0:KINDS, l, :, :]))
                step(nc.vector.tensor_tensor(bias_rest[:, :, :], biases[0:KINDS, l, :, :], bias_parts[:, 0, :, :], ALU.subtract))
                step(nc.vector.tensor_copy(bias_parts[:, 1, :, :], bias_rest[:, :, :]))
                step(nc.vector.tensor_tensor(bias_parts[:, 2, :, :], bias_rest[:, :, :], bias_parts[:, 1, :, :], ALU.subtract))
                step(nc.vector.tensor_scalar(bias_rows[:, l, :, :], bias_parts[:, 0, :, :], kind_mask[:, 0:1], None, ALU.mult))
                for p in range(1, PARTS):
                    last = nc.vector.scalar_tensor_tensor(bias_rows[:, l, :, :], bias_parts[:, p, :, :], kind_mask[:, p:p + 1],
                                                          bias_rows[:, l, :, :], ALU.mult, ALU.add)
                    step(last)
                nc.vector.tensor_tensor(b2_block[:, l, :, :], bias_rows[:, l, 1, :].unsqueeze(1).to_broadcast([KINDS, 4, D]),
                                        tile_mask[:, :].unsqueeze(2).to_broadcast([KINDS, 4, D]), ALU.mult).then_inc(biases_made, 1)

            nc.vector.tensor_reduce(tile_mask[:, :], part_mask[:, :, :], AX.X, ALU.add)
            step(nc.vector.tensor_reduce(kind_mask[:, :], part_mask[:, :, :].rearrange("r j p -> r p j"), AX.X, ALU.add))

            pair_step = vector_steps(dve, 0)
            compare(0)
            for s in range(FIRST, 0):
                pair_step(Group(0, s))
            compare(1)
            dve.wait_ge(turned, 3)
            step(nc.vector.tensor_copy(line_counts[:, :], psum[7][0:LINES, 0, COLS:COLS + 1]))
            nc.vector.memset(bad[:, 7:8], 0.0).then_inc(lines_counted, 1)
            pair_step(Group(0, 0))
            dve.wait_ge(turned, 4)
            step(nc.vector.tensor_copy(line_counts[:, :], psum[0][0:LINES, 0, 0:1]))
            nc.vector.tensor_scalar(start_table[:, :], psum[7][0:LINES, 0, 0:COLS], line_counts[:, :], None,
                                    ALU.add).then_inc(table_made, 1)
            dve.wait_ge(weights_loaded, 16 * 12)
            step(nc.vector.tensor_copy(vecs[:, 0, :, :], psum[2][:, :, :]))
            derive_weights(0)
            pair_step(Group(0, 1))
            step(nc.vector.tensor_copy(vecs[:, 1, :, :], psum[3][:, :, :]))
            dve.wait_ge(starts_in, 16)
            step(nc.vector.tensor_copy(start_f[:, :], start_row[:, :]))
            step(nc.vector.tensor_tensor(excess[:, 0, :], start_f[:, 1:NODE_TILES + 1], start_f[:, 0:NODE_TILES], ALU.subtract))
            step(nc.vector.tensor_tensor(excess[:, 1, :], start_f[:, 0:NODE_TILES], even_rate[:, :], ALU.subtract))
            step(nc.vector.tensor_reduce(bad[:, 0:2], excess[:, :, :], AX.X, ALU.max))
            step(nc.vector.tensor_scalar(bad[:, 2:3], bad[:, 0:1], float(W), None, ALU.is_le))
            step(nc.vector.tensor_scalar(bad[:, 3:4], bad[:, 1:2], float(AHEAD), bad[:, 2:3], ALU.is_le, ALU.mult))
            step(nc.vector.tensor_scalar(bad[:, 4:5], psum[4][0:1, 0, 0:1], 0.0, bad[:, 3:4], ALU.is_equal, ALU.mult))
            step(nc.vector.tensor_copy(flag[:, :], bad[:, FLAG:FLAG + 1]))
            for s in range(2, EARLY):
                pair_step(Group(0, s))
            dve.wait_ge(consts_set, CONSTS)
            dve.wait_ge(cols_made, 6)
            nc.vector.memset(g_root[:, :], 0.0).then_inc(setup_done, 3)
            dve.wait_ge(setup_done, 3)
            nc.vector.memset(bad[:, 6:7], 0.0).then_inc(flag_made, 1)
            dve.wait_ge(flag_made, 1)
            ok = dve.value_load(flag[0:1, 0:1], min_val=0, max_val=1)
            setup_steps = hands[0]
            with dve.If(ok == 1):
                run_steps(dve, pair_step, EARLY)
                derive_weights(1)
                run_steps(dve, vector_steps(dve, 1), FIRST)
            hands[0] = setup_steps
            with dve.Else():
                derive_weights(1)
                vector_general(dve)

        @block.tensor
        def _(pe):
            pe.wait_ge(masks_made, MASKS)
            pe.wait_ge(edges_cast, 1)
            for k in range(2):
                for c in range(2):
                    last = nc.tensor.transpose(psum[k][:, c, 0:PAIRS], edge_rows_f[:, c, k * P:k * P + P],
                                               ident[0:PAIRS, 0:PAIRS])
            last.then_inc(turned, 1)
            pe.wait_ge(consts_set, CONSTS)
            pe.wait_ge(weights_loaded, 16 * 12)
            for l in range(2):
                nc.tensor.matmul(psum[2 + l][:, :, :], ones_row[0:1, :], vec_row[0:1, l, :, :], start=True, stop=True)
            pe.wait_ge(downs_made, 1)
            nc.tensor.matmul(psum[4][0:1, 0, 0:1], downs[:, :], ones_col[0:PAIRS, :], start=True, stop=True).then_inc(turned, 1)
            pair_step = tensor_steps(pe, 0)
            for t in range(EDGE_TILES):
                if t % PAIRS == 0:
                    pe.wait_ge(counted, t // PAIRS + 2)
                last = nc.tensor.matmul(psum[7][0:LINES, 0, 0:COLS + 1], in_line[:, t, :], below_col[:, t, :], start=(t == 0),
                                        stop=(t == EDGE_TILES - 1))
            last.then_inc(turned, 1)
            pe.wait_ge(lines_counted, 1)
            nc.tensor.matmul(psum[0][0:LINES, 0, 0:1], lower_lines[:, :], line_counts[:, :], start=True,
                             stop=True).then_inc(turned, 1)
            for s in range(FIRST, EARLY):
                pair_step(Group(0, s))
            pe.sem_inc(early_done, 1)
            pe.wait_ge(flag_made, 1)
            ok = pe.value_load(flag[0:1, 0:1], min_val=0, max_val=1)
            with pe.If(ok == 1):
                run_steps(pe, pair_step, EARLY)
                run_steps(pe, tensor_steps(pe, 1), FIRST)
            with pe.Else():
                tensor_general(pe)



def kernel(x, src, dst, L0_gnn_W1_0, L0_gnn_b1_0, L0_gnn_W2_0, L0_gnn_b2_0, L0_gnn_ln_g0, L0_gnn_ln_b0,
           L0_gnn_W1_1, L0_gnn_b1_1, L0_gnn_W2_1, L0_gnn_b2_1, L0_gnn_ln_g1, L0_gnn_ln_b1):
    import numpy as _np
    import concourse.bacc as _bacc
    from concourse.bass_utils import run_bass_kernel_spmd as _run

    given = dict(x=x, src=src, dst=dst, W1_0=L0_gnn_W1_0, b1_0=L0_gnn_b1_0, W2_0=L0_gnn_W2_0, b2_0=L0_gnn_b2_0,
                 g_0=L0_gnn_ln_g0, b_0=L0_gnn_ln_b0, W1_1=L0_gnn_W1_1, b1_1=L0_gnn_b1_1, W2_1=L0_gnn_W2_1,
                 b2_1=L0_gnn_b2_1, g_1=L0_gnn_ln_g1, b_1=L0_gnn_ln_b1)
    nc = _bacc.Bacc("TRN2", target_bir_lowering=False, num_devices=1)
    arrays, aps = {}, {}
    for name, a in given.items():
        a = _np.ascontiguousarray(a)
        arrays[f"in_{name}"] = a
        aps[name] = nc.dram_tensor(f"in_{name}", a.shape, mybir.dt.from_np(a.dtype), kind="ExternalInput").ap()
    out = nc.dram_tensor("out", list(aps["x"].shape), F32, kind="ExternalOutput").ap()
    weights = [tuple(aps[f"{v}_{l}"] for v in ("W1", "b1", "W2", "b2", "g", "b")) for l in range(2)]
    build(nc, aps["x"], aps["src"], aps["dst"], weights, out)
    r = _run(nc, [arrays], core_ids=[0])
    return r.results[0]["out"]
```
